# Optimizing a Trainium2 kernel written in Bass

```python
import numpy as np
import jax
import jax.numpy as jnp

def _softmax(x, axis=-1):
    return jax.nn.softmax(x, axis=axis)

def _gelu(x):
    return jax.nn.gelu(x, approximate=True)

def _silu(x):
    return jax.nn.silu(x)

def _sigmoid(x):
    return jax.nn.sigmoid(x)

def _layernorm(x, axis=-1, eps=1e-05):
    m = jnp.mean(x, axis=axis, keepdims=True)
    v = jnp.var(x, axis=axis, keepdims=True)
    return (x - m) / jnp.sqrt(v + eps)

def _scatter_add(tgt, idx, src, axis=0):
    return tgt.at[idx].add(src)

def _segment_sum(src, seg, n):
    return jax.ops.segment_sum(src, seg, n)
kernel_name = 'mk_macaron_d1_jaxref_r8_e9ecdd'

def setup_inputs(seed: int=0):
    np.random.seed(seed)
    _w = jnp.asarray

    def _L0_attn_setup():
        import jax, jax.numpy as jnp
        import numpy as np
        EPS = 1e-05
        key = jax.random.key(seed)
        ks = jax.random.split(key, 7)
        B, T, H = (4, 512, 128)
        x = jax.random.normal(ks[0], (B, T, H), dtype=jnp.float32)
        gamma = jnp.ones((H,), dtype=jnp.float32)
        beta = jnp.zeros((H,), dtype=jnp.float32)
        s = 1.0 / np.sqrt(H)
        Wg = jax.random.uniform(ks[1], (H, H), minval=-s, maxval=s, dtype=jnp.float32)
        bg = jax.random.uniform(ks[2], (H,), minval=-s, maxval=s, dtype=jnp.float32)
        Wc = jax.random.uniform(ks[3], (H, H), minval=-s, maxval=s, dtype=jnp.float32)
        bc = jax.random.uniform(ks[4], (H,), minval=-s, maxval=s, dtype=jnp.float32)
        return {'x': x, 'gamma': gamma, 'beta': beta, 'Wg': Wg, 'bg': bg, 'Wc': Wc, 'bc': bc}
    _L0_attn_in = _L0_attn_setup()

    def _L0_ffn_setup():
        import jax, jax.numpy as jnp
        import numpy as np
        import math
        N_EMBD = 128
        HIDDEN = 4 * N_EMBD
        N_EXPERTS = 8
        TOP_K = 2
        B, T = (4, 256)

        def new_gelu(x):
            c = math.sqrt(2.0 / math.pi)
            return 0.5 * x * (1.0 + jnp.tanh(c * (x + 0.044715 * x * x * x)))

        def _moe_forward(x, Wfc_s, bfc_s, Wproj_s, bproj_s, Wr, Wfc, bfc, Wproj, bproj):
            Bb, Tt, C = x.shape
            xf = x.reshape(Bb * Tt, C)
            N = Bb * Tt
            shared = new_gelu(xf @ Wfc_s + bfc_s) @ Wproj_s + bproj_s
            logits = xf @ Wr
            probs = jax.nn.softmax(logits, axis=-1)
            topk_p, topk_i = jax.lax.top_k(probs, TOP_K)
            topk_p = topk_p / jnp.sum(topk_p, axis=-1, keepdims=True)
            gate = jnp.zeros((N, N_EXPERTS), dtype=xf.dtype)
            gate = gate.at[jnp.arange(N)[:, None], topk_i].add(topk_p)
            routed = jnp.zeros_like(xf)
            for e in range(N_EXPERTS):
                h = new_gelu(xf @ Wfc[e] + bfc[e]) @ Wproj[e] + bproj[e]
                routed = routed + h * gate[:, e:e + 1]
            return (shared + routed).reshape(Bb, Tt, C)
        key = jax.random.key(seed)
        ks = jax.random.split(key, 10)
        s = 0.02
        return {'x': jax.random.normal(ks[0], (B, T, N_EMBD), dtype=jnp.float32), 'Wfc_s': jax.random.normal(ks[1], (N_EMBD, HIDDEN), dtype=jnp.float32) * s, 'bfc_s': jnp.zeros((HIDDEN,), dtype=jnp.float32), 'Wproj_s': jax.random.normal(ks[2], (HIDDEN, N_EMBD), dtype=jnp.float32) * s, 'bproj_s': jnp.zeros((N_EMBD,), dtype=jnp.float32), 'Wr': jax.random.normal(ks[3], (N_EMBD, N_EXPERTS), dtype=jnp.float32) * s, 'Wfc': jax.random.normal(ks[4], (N_EXPERTS, N_EMBD, HIDDEN), dtype=jnp.float32) * s, 'bfc': jnp.zeros((N_EXPERTS, HIDDEN), dtype=jnp.float32), 'Wproj': jax.random.normal(ks[5], (N_EXPERTS, HIDDEN, N_EMBD), dtype=jnp.float32) * s, 'bproj': jnp.zeros((N_EXPERTS, N_EMBD), dtype=jnp.float32)}
    _L0_ffn_in = _L0_ffn_setup()
    _d = {'L0_attn_x': _L0_attn_in['x'], 'L0_attn_gamma': _L0_attn_in['gamma'], 'L0_attn_beta': _L0_attn_in['beta'], 'L0_attn_Wg': _L0_attn_in['Wg'], 'L0_attn_bg': _L0_attn_in['bg'], 'L0_attn_Wc': _L0_attn_in['Wc'], 'L0_attn_bc': _L0_attn_in['bc'], 'L0_ffn_Wfc_s': _L0_ffn_in['Wfc_s'], 'L0_ffn_bfc_s': _L0_ffn_in['bfc_s'], 'L0_ffn_Wproj_s': _L0_ffn_in['Wproj_s'], 'L0_ffn_bproj_s': _L0_ffn_in['bproj_s'], 'L0_ffn_Wr': _L0_ffn_in['Wr'], 'L0_ffn_Wfc': _L0_ffn_in['Wfc'], 'L0_ffn_bfc': _L0_ffn_in['bfc'], 'L0_ffn_Wproj': _L0_ffn_in['Wproj'], 'L0_ffn_bproj': _L0_ffn_in['bproj']}
    _x0 = _d['L0_attn_x']
    _d['L0_attn_x'] = jax.random.normal(jax.random.fold_in(jax.random.key(seed), 1), (4, 512, 128), dtype=_x0.dtype)
    del _x0
    return _d

def reference(L0_attn_x, L0_attn_gamma, L0_attn_beta, L0_attn_Wg, L0_attn_bg, L0_attn_Wc, L0_attn_bc, L0_ffn_Wfc_s, L0_ffn_bfc_s, L0_ffn_Wproj_s, L0_ffn_bproj_s, L0_ffn_Wr, L0_ffn_Wfc, L0_ffn_bfc, L0_ffn_Wproj, L0_ffn_bproj):

    def _L0_attn_ref(x, gamma, beta, Wg, bg, Wc, bc):
        import jax, jax.numpy as jnp
        import numpy as np
        EPS = 1e-05
        mu = jnp.mean(x, axis=-1, keepdims=True)
        var = jnp.mean((x - mu) ** 2, axis=-1, keepdims=True)
        normed = (x - mu) * jax.lax.rsqrt(var + EPS) * gamma + beta
        z = jax.nn.sigmoid(jnp.einsum('bth,oh->bto', normed, Wg) + bg)
        c = jnp.einsum('bth,oh->bto', normed, Wc) + bc
        B, T, H = x.shape

        def step(h, zc):
            z_t, c_t = zc
            h = (1.0 - z_t) * h + z_t * c_t
            return (h, h)
        h0 = jnp.zeros((B, H), dtype=x.dtype)
        _, hs = jax.lax.scan(step, h0, (jnp.swapaxes(z, 0, 1), jnp.swapaxes(c, 0, 1)))
        return jnp.swapaxes(hs, 0, 1) + x

    def _L0_ffn_ref(x, Wfc_s, bfc_s, Wproj_s, bproj_s, Wr, Wfc, bfc, Wproj, bproj):
        import jax, jax.numpy as jnp
        import numpy as np
        import math
        N_EMBD = 128
        HIDDEN = 4 * N_EMBD
        N_EXPERTS = 8
        TOP_K = 2
        B, T = (4, 256)

        def new_gelu(x):
            c = math.sqrt(2.0 / math.pi)
            return 0.5 * x * (1.0 + jnp.tanh(c * (x + 0.044715 * x * x * x)))

        def _moe_forward(x, Wfc_s, bfc_s, Wproj_s, bproj_s, Wr, Wfc, bfc, Wproj, bproj):
            Bb, Tt, C = x.shape
            xf = x.reshape(Bb * Tt, C)
            N = Bb * Tt
            shared = new_gelu(xf @ Wfc_s + bfc_s) @ Wproj_s + bproj_s
            logits = xf @ Wr
            probs = jax.nn.softmax(logits, axis=-1)
            topk_p, topk_i = jax.lax.top_k(probs, TOP_K)
            topk_p = topk_p / jnp.sum(topk_p, axis=-1, keepdims=True)
            gate = jnp.zeros((N, N_EXPERTS), dtype=xf.dtype)
            gate = gate.at[jnp.arange(N)[:, None], topk_i].add(topk_p)
            routed = jnp.zeros_like(xf)
            for e in range(N_EXPERTS):
                h = new_gelu(xf @ Wfc[e] + bfc[e]) @ Wproj[e] + bproj[e]
                routed = routed + h * gate[:, e:e + 1]
            return (shared + routed).reshape(Bb, Tt, C)
        return _moe_forward(x, Wfc_s, bfc_s, Wproj_s, bproj_s, Wr, Wfc, bfc, Wproj, bproj)
    x = L0_attn_x
    x = x + 0.5 * _L0_ffn_ref(_layernorm(x, axis=-1), L0_ffn_Wfc_s, L0_ffn_bfc_s, L0_ffn_Wproj_s, L0_ffn_bproj_s, L0_ffn_Wr, L0_ffn_Wfc, L0_ffn_bfc, L0_ffn_Wproj, L0_ffn_bproj)
    x = x + _L0_attn_ref(_layernorm(x, axis=-1), L0_attn_gamma, L0_attn_beta, L0_attn_Wg, L0_attn_bg, L0_attn_Wc, L0_attn_bc)
    x = x + 0.5 * _L0_ffn_ref(_layernorm(x, axis=-1), L0_ffn_Wfc_s, L0_ffn_bfc_s, L0_ffn_Wproj_s, L0_ffn_bproj_s, L0_ffn_Wr, L0_ffn_Wfc, L0_ffn_bfc, L0_ffn_Wproj, L0_ffn_bproj)
    return x

_drawn_inputs = setup_inputs


def setup_inputs(seed=0):
    import zlib

    import numpy as np

    out = dict(_drawn_inputs(seed))
    spreads = {'L0_attn_gamma': (1.0, 0.2),
     'L0_attn_beta': (0.0, 0.283),
     'L0_ffn_bfc_s': (0.0, 0.404),
     'L0_ffn_bproj_s': (0.0, 0.1),
     'L0_ffn_bfc': (0.0, 0.652),
     'L0_ffn_bproj': (0.0, 0.1)}
    factors = {'L0_attn_bg': 8.0}
    for name, (base, spread) in spreads.items():
        noise = np.random.default_rng([zlib.crc32(name.encode()), seed]).standard_normal(out[name].shape)
        drawn = base * np.exp(spread * noise) if base else spread * noise
        out[name] = jnp.asarray(drawn.astype(out[name].dtype))
    for name, factor in factors.items():
        out[name] = (out[name] * factor).astype(out[name].dtype)
    return out
```

```python
from contextlib import ExitStack, contextmanager

import concourse.bass as bass
from concourse import mybir

F32 = mybir.dt.float32
F16 = mybir.dt.float16
I32 = mybir.dt.int32
ALU = mybir.AluOpType
ACT = mybir.ActivationFunctionType
AX = mybir.AxisListType
ds = bass.ds

P = 128
NB, T_SEQ, C = 4, 512, 128
N = NB * T_SEQ
NT = N // P
TG = T_SEQ // P
E = 8
HID = 512
J = HID // P
G = (2 * N + E * (P - 1)) // P
K = 2
KN = K * N
NC = K * NT
U = 3
BODIES = G // U
EPS = 1e-5
X_SCALE = 1024.0
TOP = 2.0 ** 14
TINY = 2.0 ** -40
BIG = 1e30
LAYERS = 2
assert G % U == 0 and C == P


def macaron(nc, x_in, gamma, beta, wg, bg, wc, bc, wfc_s, bfc_s, wproj_s, bproj_s, wr, wfc, bfc, wproj, bproj, out):
    x_rows = x_in.rearrange("b (t p) c -> p (b t) c", p=P)
    out_rows = out.rearrange("b (t p) c -> p (b t) c", p=P)
    xsplit_dram = [nc.dram_tensor(f"xsplit_{i}", (N, 2 * C), F16, kind="Internal").ap() for i in range(LAYERS)]
    routed_dram = [nc.dram_tensor(f"routed_{i}", (KN + G * P, C), F32, kind="Internal").ap() for i in range(LAYERS)]

    with ExitStack() as ctx:
        def sb(name, shape, dt=F32):
            return ctx.enter_context(nc.sbuf_tensor(name, shape, dt))

        def sem(name):
            return ctx.enter_context(nc.semaphore(name))

        ps = ctx.enter_context(nc.psum_tensor("ps", [P, 8 * 512], F32))

        def bank(b, n=512):
            return ps[:, b * 512:b * 512 + n]

        xs = sb("xs", [P, N])
        xn = sb("xn", [P, N])
        xatt = sb("xatt", [P, N])
        xsplit = sb("xsplit", [P, NT, 2, C], F16)
        xT = sb("xT", [P, 2, N], F16)
        xT32 = xT[:, :, :].bitcast(F32)

        wraw = sb("wraw", [P, 2 * (E + 1) * HID])
        w1raw = wraw[:, 0:(E + 1) * HID].rearrange("p (e h) -> p e h", e=E + 1)
        w2raw = wraw[:, (E + 1) * HID:].rearrange("p (e j c) -> p e j c", e=E + 1, j=J)
        w1 = sb("w1", [P, E + 1, 2, HID], F16)
        w2 = sb("w2", [P, E + 1, 2, HID], F16)
        w1f = w1[:, :, :, :].rearrange("p e s h -> p (e s h)")
        w2f = w2[:, :, :, :].rearrange("p e s h -> p (e s h)")
        wr_raw = sb("wr_raw", [P, E])
        wr16 = sb("wr16", [P, 2, E], F16)
        b1rows = sb("b1rows", [(E + 1) * J, P])
        b1T = sb("b1T", [P, (E + 1) * J])
        b2rows = sb("b2rows", [E + 1, C])
        w_att_raw = sb("w_att_raw", [P, 2, C])
        w_att = sb("w_att", [P, 2, C])
        cols = sb("cols", [P, 4])
        half_bg = sb("half_bg", [P, 1])

        ident = sb("ident", [P, P])
        ident16 = sb("ident16", [P, P], F16)
        before = sb("before", [P, P], F16)
        ones16 = sb("ones16", [P, P], F16)
        ones_row = sb("ones_row", [4, P])
        rank8 = sb("rank8", [P, E])
        lane = sb("lane", [P, P], F16)
        slot_tile = sb("slot_tile", [P, G], F16)
        pair_no = sb("pair_no", [P, NC], F16)
        own_lane = sb("own_lane", [P, 1])
        carry = sb("carry", [P, E * NT])
        spare_row = sb("spare_row", [P, G])
        minus_half = sb("minus_half", [P, NT])

        bn = sb("bn", [P, NT, 6])
        ln_d = sb("ln_d", [P, 4, NT])
        mean = sb("mean", [P, NT])
        var = sb("var", [P, NT])
        veps = sb("veps", [P, NT])
        rstd = sb("rstd", [P, NT])

        peak = sb("peak", [P, 6])
        peak_max = sb("peak_max", [4, 1])
        peak_diag = sb("peak_diag", [4, 4])
        peak_all = sb("peak_all", [P, 6])
        pow2 = sb("pow2", [P, 8])
        inv = sb("inv", [P, 8])
        scale_w = sb("scale_w", [P, 8])
        un = sb("un", [P, 8])

        logits = sb("logits", [P, NT, E])
        logits2 = sb("logits2", [P, NT, E])
        pick = sb("pick", [P, 3, NT * E])
        best = sb("best", [P, K, NT])
        top_rank = sb("top_rank", [P, NT])
        chosen = sb("chosen", [P, K, NT, E])
        gap = sb("gap", [P, NT])
        gap_tanh = sb("gap_tanh", [P, NT])
        gate = sb("gate", [P, K, NT])
        gate_un = sb("gate_un", [P, K, NT])
        gates = sb("gates", [P, NT, E + 1])
        gates_k = sb("gates_k", [P, K, NT, E])
        gatesT = sb("gatesT", [E + 1, N])
        used = sb("used", [P, E * NT], F16)
        upto = sb("upto", [P, E * NT])
        ahead = sb("ahead", [P, E * NT], F16)
        total = sb("total", [P, E], F16)
        tiles_i = sb("tiles_i", [P, 2, E], I32)
        tiles = sb("tiles", [P, E])
        tile_end = sb("tile_end", [P, E])
        tile_start = sb("tile_start", [P, E])
        ones8 = sb("ones8", [P, E])
        slot_of = sb("slot_of", [P, E * NT])
        slot_k = sb("slot_k", [P, K, NT * E])
        slot = sb("slot", [P, NC])
        slot_i = sb("slot_i", [P, 3, NC], I32)
        slot_g = sb("slot_g", [P, NC], F16)
        slot_p = sb("slot_p", [P, NC], F16)
        in_lane = sb("in_lane", [P, NC, P], F16)
        in_tile = sb("in_tile", [P, NC, G], F16)
        in_tile_id = sb("in_tile_id", [P, NC, 2, G], F16)
        held = sb("held", [P, 2, G])
        row_id = sb("row_id", [P, G])
        rt = sb("rt", [P, 5, G])
        ended = sb("ended", [P, G, E])
        gather_row = sb("gather_row", [P, G], I32)
        scatter_row = sb("scatter_row", [P, G], I32)
        tile_expert = sb("tile_expert", [P, G], I32)

        h_sh = sb("h_sh", [P, J, T_SEQ])
        hs_sh = sb("hs_sh", [P, 2, J, T_SEQ], F16)
        xg = sb("xg", [P, G * 2 * C], F16)
        routed = wraw[:, 0:K * N]
        xgT = sb("xgT", [P, U, 2 * P], F16)
        h = sb("h", [P, U, HID])
        hs = sb("hs", [P, U, 2, HID], F16)
        y = sb("y", [P, U, C])

        att = wraw[:, 0:5 * 2 * T_SEQ].rearrange("p (k b t) -> p k b t", k=5, b=2)
        normT, zt, at_, bt, ht = (att[:, k] for k in range(5))

        x_loaded = sem("x_loaded")
        small_loaded = sem("small_loaded")
        shared_loaded = sem("shared_loaded")
        routed_loaded = sem("routed_loaded")
        consts_made = sem("consts_made")
        pool_step = sem("pool_step")
        dve_step = sem("dve_step")
        var_ready = sem("var_ready")
        rstd_ready = sem("rstd_ready")
        peaks_ready = sem("peaks_ready")
        peaksT_ready = sem("peaksT_ready")
        peak_diag_ready = sem("peak_diag_ready")
        peaks_spread = sem("peaks_spread")
        att_w_turned = sem("att_w_turned")
        scales_ready = sem("scales_ready")
        weights_hi = sem("weights_hi")
        router_w_ready = sem("router_w_ready")
        weights_split = sem("weights_split")
        xsplit_ready = sem("xsplit_ready")
        xsplit_stored = sem("xsplit_stored")
        xT_turned = sem("xT_turned")
        xT_ready = sem("xT_ready")
        logits_ready = sem("logits_ready")
        used_ready = sem("used_ready")
        rank_ready = sem("rank_ready")
        gap_ready = sem("gap_ready")
        gap_tanh_ready = sem("gap_tanh_ready")
        onehots_ready = sem("onehots_ready")
        held_ready = sem("held_ready")
        rows_ready = sem("rows_ready")
        experts_ready = sem("experts_ready")
        gates_ready = sem("gates_ready")
        gates_turned = sem("gates_turned")
        gatesT_ready = sem("gatesT_ready")
        bias_ready = sem("bias_ready")
        banks_read = sem("banks_read")
        sh_up = sem("sh_up")
        sh_gelu = sem("sh_gelu")
        sh_split = sem("sh_split")
        sh_down = sem("sh_down")
        gathered = [sem(f"gathered_{k}") for k in range(U)]
        scattered = [sem(f"scattered_{k}") for k in range(U)]
        xg_turned = sem("xg_turned")
        xgT_ready = sem("xgT_ready")
        up_ready = sem("up_ready")
        gelu_ready = sem("gelu_ready")
        split_ready = sem("split_ready")
        down_ready = sem("down_ready")
        y_ready = sem("y_ready")
        routed_back = sem("routed_back")
        x_ready = sem("x_ready")
        norm_ready = sem("norm_ready")
        norm_turned = sem("norm_turned")
        normT_ready = sem("normT_ready")
        gates_in = sem("gates_in")
        cand_in = sem("cand_in")
        tanh_ready = sem("tanh_ready")
        z_ready = sem("z_ready")
        hT_ready = sem("hT_ready")
        h_turned = sem("h_turned")
        x_sum_ready = sem("x_sum_ready")
        att_done = sem("att_done")
        out_stored = sem("out_stored")

        SMALL = 10
        block = ctx.enter_context(nc.Block())

        class Steps:

            def __init__(self, eng, own_sem):
                self.eng, self.own_sem, self.count, self.moving = eng, own_sem, 0, 0

            def link(self, ins):
                ins.then_inc(self.own_sem, 1)
                self.count += 1
                self.eng.wait_ge(self.own_sem, self.moving + self.count)

            @contextmanager
            def loop(self, trips, links):
                start = self.count
                with self.eng.Fori(0, trips) as i:
                    self.moving = i * links
                    yield i
                self.moving = 0
                assert self.count == start + links, (self.count - start, links)
                self.count = start + trips * links

        @block.sync
        def _(sp):
            sp.dma_start(xs[:, :].rearrange("p (t c) -> p t c", c=C), x_rows).then_inc(x_loaded, 16)
            sp.dma_start(w1raw[:, E, :], wfc_s).then_inc(shared_loaded, 16)
            sp.dma_start(w2raw[:, E], wproj_s.rearrange("(j p) c -> p j c", p=P)).then_inc(shared_loaded, 16)
            sp.dma_start(w1raw[:, 0:E], wfc.rearrange("e c h -> c e h")).then_inc(routed_loaded, 16)
            sp.dma_start(w2raw[:, 0:E], wproj.rearrange("e (j p) c -> p e j c", p=P)).then_inc(routed_loaded, 16)
            for layer in range(LAYERS):
                with sp.Fori(0, NB) as g:
                    sp.wait_ge(xsplit_ready, layer * NB + g + 1)
                    sp.dma_start(xsplit_dram[layer][ds(g * T_SEQ, T_SEQ), :].rearrange("(t p) c -> p t c", p=P),
                                 xsplit[:, ds(g * TG, TG)].rearrange("p t s c -> p t (s c)")).then_inc(xsplit_stored, 16)
                for k in range(U):
                    sp.wait_ge(scattered[k], 16 * BODIES * (layer + 1))
                for k in range(K):
                    sp.dma_start(routed[:, k * N:(k + 1) * N].rearrange("p (t c) -> p t c", c=C),
                                 routed_dram[layer][k * N:(k + 1) * N, :].rearrange("(t p) c -> p t c", p=P)
                                 ).then_inc(routed_back, 16)
            with sp.Fori(0, NB) as g:
                sp.wait_ge(x_ready, NB + g + 1)
                sp.dma_start(out_rows[:, ds(g * TG, TG), :],
                             xs[:, ds(g * T_SEQ, T_SEQ)].rearrange("p (t c) -> p t c", c=C)).then_inc(out_stored, 16)
            sp.wait_ge(out_stored, 16 * NB)
            sp.wait_ge(xsplit_stored, 16 * NB * LAYERS)

        @block.gpsimd
        def _(pool):
            steps = Steps(pool, pool_step)
            pool.memset(ident[:, :], 0.0)
            pool.memset(before[:, :], 1.0)
            pool.memset(ones16[:, :], 1.0)
            pool.memset(ones_row[:, :], 1.0)
            pool.memset(ones8[:, :], 1.0)
            pool.memset(carry[:, :], 1.0)
            pool.memset(minus_half[:, :], -0.5)
            pool.memset(peak[:, :], 0.0)
            pool.memset(gates[:, :, E:E + 1], 0.5)
            pool.iota(rank8[:, :], [[-1, E]], base=E, channel_multiplier=0, allow_small_or_imprecise_dtypes=True)
            pool.iota(lane[:, :], [[1, P]], base=0, channel_multiplier=0, allow_small_or_imprecise_dtypes=True)
            pool.iota(slot_tile[:, :], [[1, G]], base=0, channel_multiplier=0, allow_small_or_imprecise_dtypes=True)
            pool.iota(pair_no[:, :], [[1, NC]], base=1, channel_multiplier=0, allow_small_or_imprecise_dtypes=True)
            pool.iota(own_lane[:, :], [[0, 1]], base=0, channel_multiplier=1, allow_small_or_imprecise_dtypes=True)
            steps.link(pool.iota(spare_row[:, :], [[P, G]], base=KN + P, channel_multiplier=1,
                                 allow_small_or_imprecise_dtypes=True))
            pool.memset(carry[:, :].rearrange("p (e t) -> p e t", e=E)[:, :, 0:1], 0.0)
            pool.affine_select(out=before[:, :], in_=before[:, :], compare_op=ALU.is_gt, fill=0.0, base=0,
                               pattern=[[1, P]], channel_multiplier=-1)
            steps.link(pool.affine_select(out=ident[:, :], in_=ident[:, :], compare_op=ALU.not_equal, fill=1.0,
                                          base=0, pattern=[[-1, P]], channel_multiplier=1))
            pool.tensor_copy(ident16[:, :], ident[:, :]).then_inc(consts_made, 1)

            norms = [0]

            def make_rstd(scale):
                norms[0] += 1
                pool.wait_ge(var_ready, norms[0])
                steps.link(pool.tensor_scalar(veps[:, :], var[:, :], EPS, scale ** -2.0, ALU.add, ALU.mult))
                pool.tensor_tensor(rstd[:, :], veps[:, :], minus_half[:, :], ALU.pow).then_inc(rstd_ready, 1)

            for layer in range(LAYERS):
                make_rstd(X_SCALE)
                pool.wait_ge(rows_ready, layer + 1)
                pool.wait_ge(xsplit_stored, 16 * NB * (layer + 1))

                def gather(i):
                    k, n = i % U, i // U
                    if layer * BODIES + n:
                        pool.wait_ge(gathered[k], 16 * (layer * BODIES + n))
                    pool.indirect_dma_start(
                        out=xg[:, i * 2 * C:(i + 1) * 2 * C], out_offset=None, in_=xsplit_dram[layer][:, :],
                        in_offset=bass.IndirectOffsetOnAxis(ap=gather_row[:, i:i + 1], axis=0),
                    ).then_inc(gathered[k], 16)

                for i in range(2 * U):
                    gather(i)
                for i in range(G):
                    pool.wait_ge(y_ready, layer * G + i + 1)
                    pool.indirect_dma_start(
                        out=routed_dram[layer][:, :],
                        out_offset=bass.IndirectOffsetOnAxis(ap=scatter_row[:, i:i + 1], axis=0),
                        in_=y[:, i % U, :], in_offset=None,
                    ).then_inc(scattered[i % U], 16)
                    if i + 2 * U < G:
                        gather(i + 2 * U)
                if layer == 0:
                    make_rstd(1.0)
                    make_rstd(1.0)
                    for b in range(NB):
                        par = b % 2
                        at = slice(b * T_SEQ, (b + 1) * T_SEQ)
                        pool.tensor_tensor(xs[:, at], xs[:, at], xatt[:, at], ALU.add).then_inc(x_sum_ready, 1)
                        pool.wait_ge(tanh_ready, b + 1)
                        pool.tensor_scalar(at_[:, par], zt[:, par], -0.5, 0.5, ALU.mult, ALU.add)
                        pool.tensor_scalar(zt[:, par], zt[:, par], 0.5, 0.5, ALU.mult, ALU.add).then_inc(z_ready, 1)

        @block.scalar
        def _(act):
            small = [(wr_raw[:, :], wr), (b1rows[0:E * J, :], bfc.rearrange("e (j p) -> (e j) p", p=P)),
                     (b1rows[E * J:, :], bfc_s.rearrange("(j p) -> j p", p=P)), (b2rows[0:E, :], bproj),
                     (b2rows[E:E + 1, :], bproj_s.rearrange("(a c) -> a c", a=1)),
                     (w_att_raw[:, 0], wg), (w_att_raw[:, 1], wc)]
            small += [(cols[:, n:n + 1], v.rearrange("(p a) -> p a", a=1)) for n, v in enumerate((gamma, beta, bg))]
            assert len(small) == SMALL
            for dst, src in small:
                act.dma_start(dst, src).then_inc(small_loaded, 16)
            act.dma_start(cols[:, 3:4], bc.rearrange("(p a) -> p a", a=1)).then_inc(small_loaded, 16)
            act.preload_act_table(ACT.Gelu_apprx_tanh)

            for layer in range(LAYERS):
                with act.Fori(0, NB) as g:
                    act.wait_ge(xT_turned, layer * NB + g + 1)
                    act.copy(xT32[:, :, ds(g * (T_SEQ // 2), T_SEQ // 2)],
                             ps[:, ds(g * 512, 512)].rearrange("p (s t) -> p s t", s=2)).then_inc(xT_ready, 1)
                act.wait_ge(gap_ready, layer + 1)
                act.activation(gap_tanh[:, :], gap[:, :], ACT.Tanh, scale=un[:, 5:6]).then_inc(gap_tanh_ready, 1)
                if layer == 0:
                    act.wait_ge(scales_ready, 2)
                    act.activation(w1[:, 0:E, 0, :], w1raw[:, 0:E], ACT.Identity,
                                   scale=scale_w[:, 4:5]).then_inc(weights_hi, 1)
                    act.activation(w2[:, 0:E, 0, :], w2raw[:, 0:E].rearrange("p e j c -> p e (j c)"), ACT.Identity,
                                   scale=scale_w[:, 5:6]).then_inc(weights_hi, 1)
                with act.Fori(0, NB) as g:
                    for j in range(J):
                        act.wait_ge(sh_up, layer * NB * J + g * J + j + 1)
                        act.activation(h_sh[:, j, :], bank(j), ACT.Gelu_apprx_tanh, scale=un[:, 0:1],
                                       bias=b1T[:, E * J + j:E * J + j + 1]).then_inc(sh_gelu, 1)

                def gelu(i, k):
                    e = act.value_load(tile_expert[0:1, ds(i, 1)], min_val=0, max_val=E - 1)
                    act.wait_ge(up_ready, layer * G + i + 1)
                    for j in range(J):
                        ins = act.activation(h[:, k, j * P:(j + 1) * P], bank(k)[:, j * P:(j + 1) * P],
                                             ACT.Gelu_apprx_tanh, scale=un[:, 2:3], bias=b1T[:, ds(e * J + j, 1)])
                    ins.then_inc(gelu_ready, 1)

                def move_y(i, n, k):
                    act.wait_ge(down_ready, layer * G + i + 1)
                    if layer or not isinstance(n, int) or n:
                        act.wait_ge(scattered[k], 16 * (layer * BODIES + n))
                    act.copy(y[:, k, :], bank(3 + k, C)).then_inc(y_ready, 1)

                act.wait_ge(experts_ready, layer + 1)
                gelu(0, 0)
                gelu(1, 1)
                for i in range(U):
                    gelu(i + 2, (i + 2) % U)
                    move_y(i, 0, i)
                with act.Fori(1, BODIES - 1) as n:
                    for k in range(U):
                        gelu(n * U + k + 2, (k + 2) % U)
                        move_y(n * U + k, n, k)
                for i in range(G - U, G):
                    if i + 2 < G:
                        gelu(i + 2, (i + 2) % U)
                    move_y(i, i // U, i % U)

                if layer == 0:
                    with act.Fori(0, NB // 2) as m:
                        for par in range(2):
                            act.wait_ge(gates_in, 2 * m + par + 1)
                            act.activation(zt[:, par], bank(2 + par), ACT.Tanh, scale=0.5,
                                           bias=half_bg[:, 0:1]).then_inc(tanh_ready, 1)

        @block.vector
        def _(dve):
            steps = Steps(dve, dve_step)
            link = steps.link
            norms = [0]

            def statistics(src):
                with steps.loop(NB, 1) as g:
                    for t in range(TG):
                        ins = dve.bn_stats(bn[:, ds(g * TG + t, 1), :], src[:, ds(g * T_SEQ + t * C, C)])
                    link(ins)
                me, ve, mo, vo = bn[:, :, 1], bn[:, :, 2], bn[:, :, 4], bn[:, :, 5]
                dve.tensor_tensor(ln_d[:, 0, :], me, mo, ALU.subtract)
                dve.tensor_tensor(ln_d[:, 1, :], me, mo, ALU.add)
                link(dve.tensor_tensor(ln_d[:, 2, :], ve, vo, ALU.add))
                dve.tensor_scalar(mean[:, :], ln_d[:, 1, :], 0.5, None, ALU.mult)
                link(dve.scalar_tensor_tensor(ln_d[:, 3, :], ln_d[:, 0, :], 0.25, ln_d[:, 0, :], ALU.mult, ALU.mult))
                dve.scalar_tensor_tensor(var[:, :], ln_d[:, 2, :], 1.0 / C, ln_d[:, 3, :], ALU.mult,
                                         ALU.add).then_inc(var_ready, 1)
                norms[0] += 1

            def normalize(dst, src, g):
                for t in range(TG):
                    ins = dve.tensor_scalar(dst[:, ds(g * T_SEQ + t * C, C)], src[:, ds(g * T_SEQ + t * C, C)],
                                            mean[:, ds(g * TG + t, 1)], rstd[:, ds(g * TG + t, 1)],
                                            ALU.subtract, ALU.mult)
                return ins

            def spread_peaks(n, first, rnd):
                dve.wait_ge(peaksT_ready, rnd)
                link(dve.tensor_reduce(peak_max[0:n, :], bank(7)[0:n, 0:P], AX.X, ALU.max))
                dve.tensor_scalar(peak_diag[0:n, 0:n], ident[0:n, 0:n], peak_max[0:n, 0:1], None,
                                  ALU.mult).then_inc(peak_diag_ready, 1)
                dve.wait_ge(peaks_spread, rnd)
                link(dve.tensor_copy(peak_all[:, first:first + n], bank(6, n)))

            def power_of_two(dst, src):
                link(dve.tensor_scalar(dst.bitcast(I32), src.bitcast(I32), 0x7F800000, None, ALU.bitwise_and))
                link(dve.tensor_scalar(dst, dst, TINY, None, ALU.max))

            def scales(w1_, w2_, b1_, s_w, s_h, u_up, u_down):
                link(dve.scalar_tensor_tensor(pow2[:, 7:8], peak_all[:, w1_:w1_ + 1], float(P),
                                              peak_all[:, b1_:b1_ + 1], ALU.mult, ALU.add))
                power_of_two(pow2[:, 2:3], pow2[:, 7:8])
                power_of_two(pow2[:, 0:1], peak_all[:, w1_:w1_ + 1])
                power_of_two(pow2[:, 1:2], peak_all[:, w2_:w2_ + 1])
                link(dve.reciprocal(inv[:, 0:3], pow2[:, 0:3]))
                dve.tensor_scalar(scale_w[:, s_w:s_w + 2], inv[:, 0:2], TOP, None, ALU.mult)
                dve.tensor_scalar(scale_w[:, s_h:s_h + 1], inv[:, 2:3], TOP, None, ALU.mult)
                dve.tensor_scalar(un[:, u_up:u_up + 1], pow2[:, 0:1], 1.0 / (TOP * X_SCALE), None, ALU.mult)
                link(dve.scalar_tensor_tensor(un[:, u_down:u_down + 1], pow2[:, 2:3], TOP ** -2.0, pow2[:, 1:2],
                                              ALU.mult, ALU.mult))

            def first_scales():
                dve.wait_ge(consts_made, 1)
                dve.wait_ge(shared_loaded, 32)
                dve.wait_ge(small_loaded, 16 * (SMALL + 1))
                dve.tensor_reduce(peak[:, 0:1], w1raw[:, E], AX.X, ALU.max, apply_absolute_value=True)
                dve.tensor_reduce(peak[:, 1:2], w2raw[:, E].rearrange("p j c -> p (j c)"), AX.X, ALU.max,
                                  apply_absolute_value=True)
                dve.tensor_reduce(peak[:, 2:3], wr_raw[:, :], AX.X, ALU.max, apply_absolute_value=True)
                dve.tensor_reduce(peak[0:(E + 1) * J, 3:4], b1rows[:, :], AX.X, ALU.max,
                                  apply_absolute_value=True).then_inc(peaks_ready, 1)
                spread_peaks(4, 0, 1)
                scales(0, 1, 3, 0, 2, 0, 1)
                power_of_two(pow2[:, 3:4], peak_all[:, 2:3])
                link(dve.reciprocal(inv[:, 3:4], pow2[:, 3:4]))
                dve.tensor_scalar(un[:, 4:5], un[:, 1:2], 0.5, None, ALU.mult)
                dve.tensor_scalar(un[:, 5:6], pow2[:, 3:4], 0.5 / (TOP * X_SCALE), None, ALU.mult)
                link(dve.tensor_scalar(scale_w[:, 3:4], inv[:, 3:4], TOP, None, ALU.mult))
                link(dve.tensor_scalar(wr16[:, 0, :], wr_raw[:, :], scale_w[:, 3:4], None, ALU.mult))
                dve.scalar_tensor_tensor(wr16[:, 1, :], wr_raw[:, :], scale_w[:, 3:4], wr16[:, 0, :], ALU.mult,
                                         ALU.subtract).then_inc(router_w_ready, 1)
                dve.tensor_scalar(half_bg[:, :], cols[:, 2:3], 0.5, None, ALU.mult)
                dve.wait_ge(att_w_turned, 1)
                dve.tensor_copy(b1T[:, :], bank(5, (E + 1) * J))
                link(dve.tensor_copy(w_att[:, :, :].rearrange("p k c -> p (k c)"), bank(4, 2 * C)))

            def split_shared():
                for raw, w, col in ((w1raw[:, E], w1[:, E], 0),
                                    (w2raw[:, E].rearrange("p j c -> p (j c)"), w2[:, E], 1)):
                    link(dve.tensor_scalar(w[:, 0, :], raw, scale_w[:, col:col + 1], None, ALU.mult))
                    ins = dve.scalar_tensor_tensor(w[:, 1, :], raw, scale_w[:, col:col + 1], w[:, 0, :], ALU.mult,
                                                   ALU.subtract)
                ins.then_inc(weights_split, 1)

            def routed_scales():
                dve.wait_ge(routed_loaded, 32)
                dve.tensor_reduce(peak[:, 4:5], w1raw[:, 0:E].rearrange("p e h -> p (e h)"), AX.X, ALU.max,
                                  apply_absolute_value=True)
                dve.tensor_reduce(peak[:, 5:6], w2raw[:, 0:E].rearrange("p e j c -> p (e j c)"), AX.X, ALU.max,
                                  apply_absolute_value=True).then_inc(peaks_ready, 1)
                spread_peaks(2, 4, 2)
                scales(4, 5, 3, 4, 6, 2, 3)
                dve.tensor_copy(pow2[:, 6:7], pow2[:, 7:8]).then_inc(scales_ready, 2)

            def split_routed():
                dve.wait_ge(weights_hi, 1)
                dve.scalar_tensor_tensor(w1[:, 0:E, 1, :], w1raw[:, 0:E], scale_w[:, 4:5], w1[:, 0:E, 0, :],
                                         ALU.mult, ALU.subtract)
                dve.wait_ge(weights_hi, 2)
                link(dve.scalar_tensor_tensor(w2[:, 0:E, 1, :], w2raw[:, 0:E].rearrange("p e j c -> p e (j c)"),
                                              scale_w[:, 5:6], w2[:, 0:E, 0, :], ALU.mult, ALU.subtract))

            def choose(k, src):
                v = [pick[:, n, :].rearrange("p (t e) -> p t e", e=E) for n in range(2)]
                ranks = rank8[:, :].unsqueeze(1).broadcast_to([P, NT, E])
                link(dve.tensor_reduce(best[:, k, :], src, AX.X, ALU.max))
                link(dve.tensor_tensor(v[0], src, best[:, k, :].unsqueeze(2).broadcast_to([P, NT, E]), ALU.is_equal))
                link(dve.tensor_tensor(v[1], v[0], ranks, ALU.mult))
                link(dve.tensor_reduce(top_rank[:, :], v[1], AX.X, ALU.max))
                link(dve.tensor_tensor(chosen[:, k], ranks, top_rank[:, :].unsqueeze(2).broadcast_to([P, NT, E]),
                                       ALU.is_equal))

            def route(layer):
                dve.wait_ge(logits_ready, NB * (layer + 1))
                link(dve.tensor_reduce(logits[:, :, :],
                                       bank(7, NT * 2 * E).rearrange("p (t s e) -> p t e s", s=2, e=E),
                                       AX.X, ALU.add))
                choose(0, logits[:, :, :])
                link(dve.scalar_tensor_tensor(logits2[:, :, :], chosen[:, 0], -BIG, logits[:, :, :], ALU.mult,
                                              ALU.add))
                choose(1, logits2[:, :, :])
                dve.tensor_tensor(gap[:, :], best[:, 1, :], best[:, 0, :], ALU.subtract).then_inc(gap_ready, 1)
                link(dve.tensor_tensor(used[:, :].rearrange("p (e t) -> p t e", e=E), chosen[:, 0], chosen[:, 1],
                                       ALU.add))
                link(dve.tensor_tensor_scan(upto[:, :], carry[:, :], used[:, :], 0.0, ALU.mult, ALU.add))
                dve.tensor_copy(total[:, :].unsqueeze(2), upto[:, :].rearrange("p (e t) -> p e t", e=E)[:, :, NT - 1:NT])
                dve.tensor_tensor(ahead[:, :], upto[:, :], used[:, :], ALU.subtract).then_inc(used_ready, 1)
                dve.wait_ge(rank_ready, layer + 1)
                link(dve.tensor_scalar(tiles_i[:, 0, :], bank(6)[:, P:P + E], float(P - 1), None, ALU.add))
                link(dve.tensor_scalar(tiles_i[:, 1, :], tiles_i[:, 0, :], 7, None, ALU.logical_shift_right))
                link(dve.tensor_copy(tiles[:, :], tiles_i[:, 1, :]))
                link(dve.tensor_tensor_scan(tile_end[:, :], ones8[:, :], tiles[:, :], 0.0, ALU.mult, ALU.add))
                link(dve.tensor_tensor(tile_start[:, :], tile_end[:, :], tiles[:, :], ALU.subtract))
                link(dve.scalar_tensor_tensor(slot_of[:, :].rearrange("p (e t) -> p e t", e=E),
                                              tile_start[:, :].unsqueeze(2).broadcast_to([P, E, NT]), float(P),
                                              bank(6, P).rearrange("p (e t) -> p e t", e=E), ALU.mult, ALU.add))
                sk = [slot_k[:, k, :].rearrange("p (t e) -> p t e", e=E) for k in range(K)]
                for k in range(K):
                    ins = dve.tensor_tensor(sk[k], chosen[:, k], slot_of[:, :].rearrange("p (e t) -> p t e", e=E),
                                            ALU.mult)
                link(ins)
                for k in range(K):
                    ins = dve.tensor_reduce(slot[:, k * NT:(k + 1) * NT], sk[k], AX.X, ALU.add)
                link(ins)
                link(dve.tensor_copy(slot_i[:, 0, :], slot[:, :]))
                dve.tensor_scalar(slot_i[:, 1, :], slot_i[:, 0, :], 7, None, ALU.logical_shift_right)
                link(dve.tensor_scalar(slot_i[:, 2, :], slot_i[:, 0, :], P - 1, None, ALU.bitwise_and))
                dve.tensor_copy(slot_g[:, :], slot_i[:, 1, :])
                link(dve.tensor_copy(slot_p[:, :], slot_i[:, 2, :]))
                link(dve.tensor_tensor(in_tile[:, :, :], slot_tile[:, :].unsqueeze(1).broadcast_to([P, NC, G]),
                                       slot_g[:, :].unsqueeze(2).broadcast_to([P, NC, G]), ALU.is_equal))
                dve.tensor_tensor(in_tile_id[:, :, 0, :], in_tile[:, :, :],
                                  pair_no[:, :].unsqueeze(2).broadcast_to([P, NC, G]), ALU.mult)
                dve.tensor_scalar(in_tile_id[:, :, 1, :], in_tile[:, :, :], own_lane[:, 0:1], None, ALU.mult)
                dve.tensor_tensor(in_lane[:, :, :], lane[:, :].unsqueeze(1).broadcast_to([P, NC, P]),
                                  slot_p[:, :].unsqueeze(2).broadcast_to([P, NC, P]), ALU.is_equal
                                  ).then_inc(onehots_ready, 1)
                link(dve.tensor_tensor(ended[:, :, :], slot_tile[:, :].unsqueeze(2).broadcast_to([P, G, E]),
                                       tile_end[:, :].unsqueeze(1).broadcast_to([P, G, E]), ALU.is_ge))
                link(dve.tensor_reduce(rt[:, 4, :], ended[:, :, :], AX.X, ALU.add))
                dve.tensor_scalar(tile_expert[:, :], rt[:, 4, :], float(E - 1), None, ALU.min
                                  ).then_inc(experts_ready, 1)
                dve.wait_ge(held_ready, layer + 1)
                link(dve.tensor_copy(held[:, :, :].rearrange("p s g -> p (s g)"), bank(6, 2 * G)))
                link(dve.scalar_tensor_tensor(row_id[:, :], held[:, 0, :], float(P), held[:, 1, :], ALU.mult, ALU.add))
                link(dve.tensor_scalar(rt[:, 0, :], row_id[:, :], -float(P), None, ALU.add))
                dve.tensor_scalar(rt[:, 1, :], rt[:, 0, :], float(N), -float(N), ALU.is_ge, ALU.mult)
                link(dve.scalar_tensor_tensor(rt[:, 2, :], rt[:, 0, :], 0.0, spare_row[:, :], ALU.is_lt, ALU.mult))
                dve.tensor_tensor(scatter_row[:, :], rt[:, 0, :], rt[:, 2, :], ALU.add)
                link(dve.tensor_tensor(rt[:, 3, :], rt[:, 0, :], rt[:, 1, :], ALU.add))
                dve.tensor_scalar(gather_row[:, :], rt[:, 3, :], 0.0, None, ALU.max).then_inc(rows_ready, 1)

            def make_gates(layer):
                dve.wait_ge(gap_tanh_ready, layer + 1)
                dve.tensor_scalar(gate[:, 0, :], gap_tanh[:, :], -0.25, 0.25, ALU.mult, ALU.add)
                link(dve.tensor_scalar(gate[:, 1, :], gap_tanh[:, :], 0.25, 0.25, ALU.mult, ALU.add))
                for k in range(K):
                    ins = dve.tensor_tensor(gates_k[:, k], chosen[:, k],
                                            gate[:, k, :].unsqueeze(2).broadcast_to([P, NT, E]), ALU.mult)
                link(ins)
                dve.tensor_tensor(gates[:, :, 0:E], gates_k[:, 0], gates_k[:, 1], ALU.add).then_inc(gates_ready, 1)

            def add_biases(layer):
                for g in range(NB):
                    dve.wait_ge(gates_turned, layer * NB + g + 1)
                    dve.tensor_copy(gatesT[:, g * T_SEQ:(g + 1) * T_SEQ], bank(g)[0:E + 1, :]).then_inc(gatesT_ready, 1)
                for g in range(NB):
                    dve.wait_ge(bias_ready, layer * NB + g + 1)
                    ins = dve.tensor_tensor(xs[:, g * T_SEQ:(g + 1) * T_SEQ], xs[:, g * T_SEQ:(g + 1) * T_SEQ],
                                            bank(g), ALU.add)
                ins.then_inc(banks_read, 1)

            def shared(layer):
                with steps.loop(NB, J + 1) as g:
                    for j in range(J):
                        dve.wait_ge(sh_gelu, layer * NB * J + g * J + j + 1)
                        link(dve.tensor_scalar(hs_sh[:, 0, j, :], h_sh[:, j, :], scale_w[:, 2:3], None, ALU.mult))
                        dve.scalar_tensor_tensor(hs_sh[:, 1, j, :], h_sh[:, j, :], scale_w[:, 2:3], hs_sh[:, 0, j, :],
                                                 ALU.mult, ALU.subtract).then_inc(sh_split, 1)
                    dve.wait_ge(sh_down, layer * NB + g + 1)
                    dve.scalar_tensor_tensor(xs[:, ds(g * T_SEQ, T_SEQ)], bank(4), un[:, 4:5],
                                             xs[:, ds(g * T_SEQ, T_SEQ)], ALU.mult, ALU.add).then_inc(banks_read, 1)
                    link(dve.memset(ln_d[:, 0, 0:1], 0.0))

            def routed_tiles(layer):
                def move_xg(i, k):
                    dve.wait_ge(xg_turned, layer * G + i + 1)
                    dve.tensor_copy(xgT[:, k, :], bank(6, P).bitcast(F16)).then_inc(xgT_ready, 1)

                def split(i, k):
                    dve.wait_ge(gelu_ready, layer * G + i + 1)
                    link(dve.tensor_scalar(hs[:, k, 0, :], h[:, k, :], scale_w[:, 6:7], None, ALU.mult))
                    dve.scalar_tensor_tensor(hs[:, k, 1, :], h[:, k, :], scale_w[:, 6:7], hs[:, k, 0, :],
                                             ALU.mult, ALU.subtract).then_inc(split_ready, 1)

                for i in range(U):
                    move_xg(i, i)
                with steps.loop(BODIES - 1, U) as n:
                    for k in range(U):
                        split(n * U + k, k)
                        move_xg(n * U + k + U, k)
                for i in range(G - U, G):
                    split(i, i % U)

            def combine(layer):
                dve.wait_ge(routed_back, 16 * K * (layer + 1))
                with steps.loop(NB, 1) as g:
                    for k in range(K):
                        for t in range(TG):
                            at = ds(g * T_SEQ + t * C, C)
                            ins = dve.scalar_tensor_tensor(
                                xs[:, at], routed[:, ds(k * N + g * T_SEQ + t * C, C)],
                                gate_un[:, k, ds(g * TG + t, 1)], xs[:, at], ALU.mult, ALU.add)
                        if k == 0:
                            link(ins)
                    ins.then_inc(x_ready, 1)
                dve.wait_ge(x_ready, NB * (layer + 1))

            def gru():
                statistics(xs)
                dve.wait_ge(rstd_ready, norms[0])
                with steps.loop(NB, 1) as g:
                    link(normalize(xatt, xs, g))
                statistics(xatt)
                dve.wait_ge(rstd_ready, norms[0])
                with dve.Fori(0, NB) as g:
                    normalize(xn, xatt, g).then_inc(norm_ready, 1)
                with steps.loop(NB // 2, 2 * 2) as m:
                    for par in range(2):
                        b = 2 * m + par
                        dve.wait_ge(norm_turned, b + 1)
                        dve.tensor_scalar(normT[:, par], bank(par), cols[:, 0:1], cols[:, 1:2], ALU.mult,
                                          ALU.add).then_inc(normT_ready, 1)
                        dve.wait_ge(cand_in, b + 1)
                        dve.wait_ge(z_ready, b + 1)
                        link(dve.scalar_tensor_tensor(bt[:, par], bank(4 + par), cols[:, 3:4], zt[:, par],
                                                      ALU.add, ALU.mult))
                        dve.tensor_tensor_scan(ht[:, par], at_[:, par], bt[:, par], 0.0, ALU.mult,
                                               ALU.add).then_inc(hT_ready, 1)
                        dve.wait_ge(h_turned, b + 1)
                        dve.wait_ge(x_sum_ready, b + 1)
                        link(dve.tensor_tensor(xs[:, ds(b * T_SEQ, T_SEQ)], bank(6 + par),
                                               xs[:, ds(b * T_SEQ, T_SEQ)], ALU.add))

            first_scales()
            dve.wait_ge(x_loaded, 16)
            for layer in range(LAYERS):
                statistics(xs)
                dve.wait_ge(rstd_ready, norms[0])
                with steps.loop(NB, 2) as g:
                    link(normalize(xn, xs, g))
                    rows = xn[:, ds(g * T_SEQ, T_SEQ)].rearrange("p (t c) -> p t c", c=C)
                    link(dve.tensor_copy(xsplit[:, ds(g * TG, TG), 0, :], rows))
                    dve.tensor_tensor(xsplit[:, ds(g * TG, TG), 1, :], rows, xsplit[:, ds(g * TG, TG), 0, :],
                                      ALU.subtract).then_inc(xsplit_ready, 1)
                route(layer)
                make_gates(layer)
                if layer == 0:
                    split_shared()
                    routed_scales()
                    split_routed()
                link(dve.tensor_scalar(gate_un[:, :, :], gate[:, :, :], un[:, 3:4], None, ALU.mult))
                add_biases(layer)
                dve.wait_ge(banks_read, layer * (NB + 1) + 1)
                shared(layer)
                routed_tiles(layer)
                combine(layer)
                if layer == 0:
                    gru()

        @block.tensor
        def _(pe):
            def transpose_peaks(n, first, rnd):
                pe.wait_ge(peaks_ready, rnd)
                pe.transpose(bank(7)[0:n, 0:P], peak[:, first:first + n], ident[:, :]).then_inc(peaksT_ready, 1)
                pe.wait_ge(peak_diag_ready, rnd)
                pe.matmul(bank(6, n), ones_row[0:n, :], peak_diag[0:n, 0:n], start=True,
                          stop=True).then_inc(peaks_spread, 1)

            def three(out, wh, wl, xh, xl, first, last):
                pe.matmul(out, wh, xh, start=first, stop=False, skip_group_check=True)
                pe.matmul(out, wh, xl, start=False, stop=False, skip_group_check=True)
                return pe.matmul(out, wl, xh, start=False, stop=last, skip_group_check=True)

            pe.wait_ge(consts_made, 1)
            transpose_peaks(4, 0, 1)
            pe.wait_ge(small_loaded, 16 * (SMALL + 1))
            pe.transpose(bank(5, (E + 1) * J), b1rows[:, :], ident[0:(E + 1) * J, 0:(E + 1) * J])
            pe.transpose(bank(4)[:, 0:C], w_att_raw[:, 0], ident[:, :])
            pe.transpose(bank(4)[:, C:2 * C], w_att_raw[:, 1], ident[:, :]).then_inc(att_w_turned, 1)

            for layer in range(LAYERS):
                ps16 = ps[:, :].bitcast(F16)
                if layer == 0:
                    pe.wait_ge(router_w_ready, 1)
                with pe.Fori(0, NB) as g:
                    pe.wait_ge(xsplit_ready, layer * NB + g + 1)
                    for s in range(2):
                        for t in range(TG):
                            ins = pe.transpose(ps16[:, ds(g * 1024 + s * T_SEQ + t * P, P)],
                                               xsplit[:, ds(g * TG + t, 1), s, :].rearrange("p a c -> p (a c)"),
                                               ident16[:, :])
                    ins.then_inc(xT_turned, 1)
                    pe.wait_ge(xT_ready, layer * NB + g + 1)
                    for t in range(TG):
                        at = ds(7 * 512 + (g * TG + t) * 2 * E, 2 * E)
                        pe.matmul(ps[:, at], xT[:, 0, ds(g * T_SEQ + t * P, P)],
                                  wr16[:, :, :].rearrange("p s e -> p (s e)"), start=True, stop=False)
                        ins = pe.matmul(ps[:, at], xT[:, 1, ds(g * T_SEQ + t * P, P)],
                                        wr16[:, :, :].rearrange("p s e -> p (s e)"), start=False, stop=True)
                    ins.then_inc(logits_ready, 1)
                pe.wait_ge(used_ready, layer + 1)
                pe.matmul(bank(6, P), before[:, :], used[:, :], start=True, stop=False)
                pe.matmul(bank(6, P), ones16[:, :], ahead[:, :], start=False, stop=True)
                pe.matmul(bank(6)[:, P:P + E], ones16[:, :], total[:, :], start=True, stop=True).then_inc(rank_ready, 1)
                pe.wait_ge(onehots_ready, layer + 1)
                for n in range(NC):
                    ins = pe.matmul(bank(6, 2 * G), in_lane[:, n, :], in_tile_id[:, n].rearrange("p s g -> p (s g)"),
                                    start=(n == 0), stop=(n == NC - 1))
                ins.then_inc(held_ready, 1)
                if layer == 0:
                    pe.wait_ge(gates_ready, 1)
                else:
                    pe.wait_ge(gates_ready, 2)
                for t in range(NT):
                    ins = pe.transpose(bank(t // TG)[0:E + 1, (t % TG) * P:(t % TG + 1) * P], gates[:, t, :], ident[:, :])
                    if t % TG == TG - 1:
                        ins.then_inc(gates_turned, 1)
                if layer == 0:
                    transpose_peaks(2, 4, 2)
                for t in range(NT):
                    if t % TG == 0:
                        pe.wait_ge(gatesT_ready, layer * NB + t // TG + 1)
                    ins = pe.matmul(bank(t // TG)[:, (t % TG) * P:(t % TG + 1) * P], gatesT[:, t * P:(t + 1) * P],
                                    b2rows[:, :], start=True, stop=True)
                    if t % TG == TG - 1:
                        ins.then_inc(bias_ready, 1)
                if layer == 0:
                    pe.wait_ge(weights_split, 1)

                with pe.Fori(0, NB) as g:
                    pe.wait_ge(banks_read, layer * (NB + 1) + g + 1)
                    for j in range(J):
                        three(bank(j), w1[:, E, 0, j * P:(j + 1) * P], w1[:, E, 1, j * P:(j + 1) * P],
                              xT[:, 0, ds(g * T_SEQ, T_SEQ)], xT[:, 1, ds(g * T_SEQ, T_SEQ)], True,
                              True).then_inc(sh_up, 1)
                    for j in range(J):
                        pe.wait_ge(sh_split, layer * NB * J + g * J + j + 1)
                        for t in range(TG):
                            hh, hl = (hs_sh[:, s, j, t * P:(t + 1) * P] for s in range(2))
                            ins = three(bank(4)[:, t * C:(t + 1) * C], hh, hl, w2[:, E, 0, j * C:(j + 1) * C],
                                        w2[:, E, 1, j * C:(j + 1) * C], j == 0 and t == 0, j == J - 1)
                    ins.then_inc(sh_down, 1)

                def turn(i, n, k):
                    pe.wait_ge(gathered[k], 16 * (layer * BODIES + n + 1))
                    for s in range(2):
                        ins = pe.transpose(bank(6, P).bitcast(F16)[:, s * P:(s + 1) * P],
                                           xg[:, ds(i * 2 * C + s * C, C)], ident16[:, :])
                    ins.then_inc(xg_turned, 1)

                def up(i, k, e):
                    pe.wait_ge(xgT_ready, layer * G + i + 1)
                    for j in range(J):
                        wh, wl = (w1f[:, ds(e * (2 * HID) + s * HID + j * P, P)] for s in range(2))
                        ins = three(bank(k)[:, j * P:(j + 1) * P], wh, wl, xgT[:, k, 0:P], xgT[:, k, P:2 * P], True,
                                    True)
                    ins.then_inc(up_ready, 1)

                def down(i, k, e):
                    pe.wait_ge(split_ready, layer * G + i + 1)
                    for j in range(J):
                        hh, hl = (hs[:, k, s, j * P:(j + 1) * P] for s in range(2))
                        wh, wl = (w2f[:, ds(e * (2 * HID) + s * HID + j * C, C)] for s in range(2))
                        ins = three(bank(3 + k, C), hh, hl, wh, wl, j == 0, j == J - 1)
                    ins.then_inc(down_ready, 1)

                def expert(i):
                    return pe.value_load(tile_expert[0:1, ds(i, 1)], min_val=0, max_val=E - 1)

                pe.wait_ge(experts_ready, layer + 1)
                if layer == 0:
                    pe.wait_ge(weights_split, 1)
                turn(0, 0, 0)
                up(0, 0, expert(0))
                turn(1, 0, 1)
                up(1, 1, expert(1))
                turn(2, 0, 2)
                with pe.Fori(0, BODIES - 1) as n:
                    for k in range(U):
                        up(n * U + k + 2, (k + 2) % U, expert(n * U + k + 2))
                        down(n * U + k, k, expert(n * U + k))
                        turn(n * U + k + U, n + 1, k)
                for i in range(G - U, G):
                    if i + 2 < G:
                        up(i + 2, (i + 2) % U, expert(i + 2))
                    down(i, i % U, expert(i))

                if layer == 0:
                    pe.wait_ge(norm_ready, NB)
                    for b in range(NB):
                        par = b % 2
                        for t in range(TG):
                            ins = pe.transpose(bank(par)[:, t * P:(t + 1) * P],
                                               xn[:, b * T_SEQ + t * C:b * T_SEQ + (t + 1) * C], ident[:, :])
                        ins.then_inc(norm_turned, 1)
                        pe.wait_ge(normT_ready, b + 1)
                        pe.matmul(bank(2 + par), w_att[:, 0], normT[:, par], start=True, stop=True).then_inc(gates_in, 1)
                        pe.matmul(bank(4 + par), w_att[:, 1], normT[:, par], start=True, stop=True).then_inc(cand_in, 1)
                        pe.wait_ge(hT_ready, b + 1)
                        for t in range(TG):
                            ins = pe.transpose(bank(6 + par)[:, t * P:(t + 1) * P], ht[:, par, t * P:(t + 1) * P],
                                               ident[:, :])
                        ins.then_inc(h_turned, 1)


_INS = ["L0_attn_x", "L0_attn_gamma", "L0_attn_beta", "L0_attn_Wg", "L0_attn_bg", "L0_attn_Wc", "L0_attn_bc",
        "L0_ffn_Wfc_s", "L0_ffn_bfc_s", "L0_ffn_Wproj_s", "L0_ffn_bproj_s", "L0_ffn_Wr", "L0_ffn_Wfc", "L0_ffn_bfc",
        "L0_ffn_Wproj", "L0_ffn_bproj"]


def kernel(**inputs):
    import numpy as np
    import concourse.bacc as bacc
    from concourse.bass_utils import run_bass_kernel_spmd

    nc = bacc.Bacc("TRN2", target_bir_lowering=False, num_devices=1)
    arrays, args = {}, []
    for name in _INS:
        a = np.ascontiguousarray(inputs[name])
        arrays[f"in_{name}"] = a
        args.append(nc.dram_tensor(f"in_{name}", a.shape, mybir.dt.from_np(a.dtype), kind="ExternalInput").ap())
    out = nc.dram_tensor("out_x", (NB, T_SEQ, C), F32, kind="ExternalOutput").ap()
    macaron(nc, *args, out)
    r = run_bass_kernel_spmd(nc, [arrays], core_ids=[0])
    return r.results[0]["out_x"]
```

```python
from contextlib import ExitStack, contextmanager

import concourse.bass as bass
from concourse import mybir

F32 = mybir.dt.float32
F16 = mybir.dt.float16
I32 = mybir.dt.int32
BF16 = mybir.dt.bfloat16
ALU = mybir.AluOpType
ACT = mybir.ActivationFunctionType
AX = mybir.AxisListType
ds = bass.ds

P = 128
NB, T_SEQ, C = 4, 512, 128
N = NB * T_SEQ
NT = N // P
TG = T_SEQ // P
E = 8
HID = 512
J = HID // P
U = 4
G = -(-((2 * N + E * (P - 1)) // P) // U) * U
K = 2
KN = K * N
NC = K * NT
BODIES = G // U
AHEAD = 24
EPS = 1e-5
X_SCALE = 1024.0
TOP = 2.0 ** 14
TINY = 2.0 ** -40
BIG = 1e30
LAYERS = 2
assert G % U == 0 and C == P


def macaron(nc, x_in, gamma, beta, wg, bg, wc, bc, wfc_s, bfc_s, wproj_s, bproj_s, wr, wfc, bfc, wproj, bproj, out):
    x_rows = x_in.rearrange("b (t p) c -> p (b t) c", p=P)
    out_rows = out.rearrange("b (t p) c -> p (b t) c", p=P)
    xsplit_dram = [nc.dram_tensor(f"xsplit_{i}", (N, 2 * C), F16, kind="Internal").ap() for i in range(LAYERS)]
    routed_dram = [nc.dram_tensor(f"routed_{i}", (KN + G * P, C), F32, kind="Internal").ap() for i in range(LAYERS)]

    with ExitStack() as ctx:
        def sb(name, shape, dt=F32):
            return ctx.enter_context(nc.sbuf_tensor(name, shape, dt))

        def sem(name):
            return ctx.enter_context(nc.semaphore(name))

        ps = ctx.enter_context(nc.psum_tensor("ps", [P, 8 * 512], F32))

        def bank(b, n=512):
            return ps[:, b * 512:b * 512 + n]

        xs = sb("xs", [P, N])
        xn = sb("xn", [P, N])
        xatt = sb("xatt", [P, N])
        xsplit = sb("xsplit", [P, NT, 2, C], F16)
        xT = sb("xT", [P, 2, N], F16)
        xT32 = xT[:, :, :].bitcast(F32)

        wraw = sb("wraw", [P, 2 * (E + 1) * HID])
        w1raw = wraw[:, 0:(E + 1) * HID].rearrange("p (e h) -> p e h", e=E + 1)
        w2raw = wraw[:, (E + 1) * HID:].rearrange("p (e j c) -> p e j c", e=E + 1, j=J)
        w1 = sb("w1", [P, E + 1, 2, HID], F16)
        w2 = sb("w2", [P, E + 1, J, 2, C], F16)
        w1f = w1[:, :, :, :].rearrange("p e s h -> p (e s h)")
        w2f = w2[:, :, :, :, :].rearrange("p e j s c -> p (e j s c)")
        wr_raw = sb("wr_raw", [P, E])
        wr16 = sb("wr16", [P, 2, E], F16)
        b1rows = sb("b1rows", [(E + 1) * J, P])
        b1_rest = sb("b1_rest", [E * J, P])
        b1_parts = sb("b1_parts", [E * J, 3, P], BF16)
        b1_flat = sb("b1_flat", [3, E * HID], BF16)
        ones_bf = sb("ones_bf", [3, P], BF16)
        b1T = sb("b1T", [P, (E + 1) * J])
        b2rows = sb("b2rows", [E + 1, C])
        w_att_raw = sb("w_att_raw", [P, 2, C])
        w_att = sb("w_att", [P, 2, C])
        cols = sb("cols", [P, 4])
        half_bg = sb("half_bg", [P, 1])

        ident = sb("ident", [P, P])
        ident16 = sb("ident16", [P, P], F16)
        before = sb("before", [P, P], F16)
        ones16 = sb("ones16", [P, P], F16)
        ones_row = sb("ones_row", [4, P])
        rank8 = sb("rank8", [P, E])
        lane = sb("lane", [P, P], F16)
        slot_tile = sb("slot_tile", [P, G], F16)
        pair_no = sb("pair_no", [P, NC], F16)
        own_lane = sb("own_lane", [P, 1])
        carry = sb("carry", [P, E * NT])
        spare_row = sb("spare_row", [P, G])
        minus_half = sb("minus_half", [P, K, TG])

        bn = sb("bn", [P, NT, 6])
        moments = sb("moments", [P, NT, 2])
        veps = sb("veps", [P, NT])
        rstd = sb("rstd", [P, NT])
        att_v = sb("att_v", [P, 3, NT])
        att_q = sb("att_q", [P, 2, NT])
        att_r = sb("att_r", [P, 2, NT])

        peak = sb("peak", [P, 6])
        peak_max = sb("peak_max", [4, 1])
        peak_diag = sb("peak_diag", [4, 4])
        peak_all = sb("peak_all", [P, 6])
        pow2 = sb("pow2", [P, 8])
        inv = sb("inv", [P, 8])
        scale_w = sb("scale_w", [P, 8])
        un = sb("un", [P, 8])

        logits = sb("logits", [P, NT, E])
        logits2 = sb("logits2", [P, NT, E])
        pick = sb("pick", [P, 3, NT * E])
        best = sb("best", [P, K, NT])
        top_rank = sb("top_rank", [P, NT])
        chosen = sb("chosen", [P, K, NT, E])
        gap = sb("gap", [P, NT])
        gap_tanh = sb("gap_tanh", [P, NT])
        gate = sb("gate", [P, K, NT])
        gate_un = sb("gate_un", [P, K, NT])
        gates = sb("gates", [P, NT, E + 1])
        gates_k = sb("gates_k", [P, K, NT, E])
        gatesT = sb("gatesT", [E + 1, N])
        used = sb("used", [P, E * NT], F16)
        upto = sb("upto", [P, E * NT])
        ahead = sb("ahead", [P, E * NT], F16)
        total = sb("total", [P, E], F16)
        tiles_i = sb("tiles_i", [P, 2, E], I32)
        tiles = sb("tiles", [P, E])
        tile_end = sb("tile_end", [P, E])
        tile_start = sb("tile_start", [P, E])
        ones8 = sb("ones8", [P, E])
        slot_of = sb("slot_of", [P, E * NT])
        slot_k = sb("slot_k", [P, K, NT * E])
        slot = sb("slot", [P, NC])
        slot_i = sb("slot_i", [P, 3, NC], I32)
        slot_g = sb("slot_g", [P, NC], F16)
        slot_p = sb("slot_p", [P, NC], F16)
        in_lane = sb("in_lane", [P, NC, P], F16)
        in_tile = sb("in_tile", [P, NC, G], F16)
        in_tile_id = sb("in_tile_id", [P, NC, 2, G], F16)
        held = sb("held", [P, 2, G])
        row_id = sb("row_id", [P, G])
        rt = sb("rt", [P, 5, G])
        ended = sb("ended", [P, G, E])
        gather_row = sb("gather_row", [P, G], I32)
        scatter_row = sb("scatter_row", [P, G], I32)
        tile_expert = sb("tile_expert", [P, G], I32)

        h_sh = sb("h_sh", [P, J, T_SEQ])
        hs_sh = sb("hs_sh", [P, 2, J, T_SEQ], F16)
        xg = sb("xg", [P, G * 2 * C], F16)
        routed = wraw[:, 0:K * N]
        xgT = sb("xgT", [P, 2, 2 * P], F16)
        h = h_sh[:, 0:2]
        hs = hs_sh[:, :, :, :].rearrange("p s j t -> p j s t")[:, 0:2]
        y_low = sb("y_low", [P, 2, C])
        y = sb("y", [P, U, C])

        att = wraw[:, K * N:K * N + 5 * 2 * T_SEQ].rearrange("p (k b t) -> p k b t", k=5, b=2)
        normT, zt, at_, bt, ht = (att[:, k] for k in range(5))
        zh = h_sh[:, 0:2]

        x_loaded = [sem(f"x_loaded_{g}") for g in range(NB)]
        small_loaded = sem("small_loaded")
        shared_loaded = sem("shared_loaded")
        routed_loaded = sem("routed_loaded")
        consts_made = sem("consts_made")
        pool_step = sem("pool_step")
        dve_step = sem("dve_step")
        var_ready = sem("var_ready")
        rstd_ready = sem("rstd_ready")
        ln_ready = sem("ln_ready")
        ln_high = sem("ln_high")
        att_var_ready = sem("att_var_ready")
        att_rstd_ready = sem("att_rstd_ready")
        xatt_ready = sem("xatt_ready")
        peaks_ready = sem("peaks_ready")
        peaksT_ready = sem("peaksT_ready")
        peak_diag_ready = sem("peak_diag_ready")
        peaks_spread = sem("peaks_spread")
        att_w_turned = sem("att_w_turned")
        scales_ready = sem("scales_ready")
        weights_hi = sem("weights_hi")
        router_w_ready = sem("router_w_ready")
        weights_split = sem("weights_split")
        weights_low = sem("weights_low")
        xsplit_ready = sem("xsplit_ready")
        xsplit_stored = sem("xsplit_stored")
        xT_turned = sem("xT_turned")
        xT_ready = sem("xT_ready")
        logits_ready = sem("logits_ready")
        used_ready = sem("used_ready")
        rank_ready = sem("rank_ready")
        gap_ready = sem("gap_ready")
        gap_tanh_ready = sem("gap_tanh_ready")
        onehots_ready = sem("onehots_ready")
        held_ready = sem("held_ready")
        rows_ready = sem("rows_ready")
        experts_ready = sem("experts_ready")
        gates_ready = sem("gates_ready")
        gates_turned = sem("gates_turned")
        gatesT_ready = sem("gatesT_ready")
        bias_ready = sem("bias_ready")
        bias_moved = sem("bias_moved")
        bias_added = sem("bias_added")
        sh_up = sem("sh_up")
        sh_gelu = sem("sh_gelu")
        sh_high = sem("sh_high")
        sh_split = sem("sh_split")
        sh_down = sem("sh_down")
        gathered = [sem(f"gathered_{k}") for k in range(U)]
        scattered = [sem(f"scattered_{k}") for k in range(U)]
        xg_turned = sem("xg_turned")
        xgT_ready = sem("xgT_ready")
        b1_parts_ready = sem("b1_parts_ready")
        b1_flat_ready = sem("b1_flat_ready")
        h_slots_turned = sem("h_slots_turned")
        high_ready = sem("high_ready")
        y_low_ready = sem("y_low_ready")
        up_ready = sem("up_ready")
        gelu_ready = sem("gelu_ready")
        split_ready = sem("split_ready")
        down_ready = sem("down_ready")
        y_ready = sem("y_ready")
        routed_back = [sem(f"routed_back_{g}") for g in range(NB)]
        x_done = sem("x_done")
        norm_ready = sem("norm_ready")
        norm_turned = sem("norm_turned")
        normT_ready = sem("normT_ready")
        gates_in = sem("gates_in")
        cand_in = sem("cand_in")
        tanh_ready = sem("tanh_ready")
        z_ready = sem("z_ready")
        hT_ready = sem("hT_ready")
        h_turned = sem("h_turned")
        x_sum_ready = sem("x_sum_ready")
        out_stored = sem("out_stored")

        SMALL = 10
        block = ctx.enter_context(nc.Block())

        class Steps:

            def __init__(self, eng, own_sem):
                self.eng, self.own_sem, self.count, self.moving = eng, own_sem, 0, 0

            def link(self, ins):
                ins.then_inc(self.own_sem, 1)
                self.count += 1
                self.eng.wait_ge(self.own_sem, self.moving + self.count)

            @contextmanager
            def loop(self, trips, links):
                start = self.count
                with self.eng.Fori(0, trips) as i:
                    self.moving = i * links
                    yield i
                self.moving = 0
                assert self.count == start + links, (self.count - start, links)
                self.count = start + trips * links

        @block.sync
        def _(sp):
            for g in range(NB):
                sp.dma_start(xs[:, g * T_SEQ:(g + 1) * T_SEQ].rearrange("p (t c) -> p t c", c=C),
                             x_rows[:, g * TG:(g + 1) * TG]).then_inc(x_loaded[g], 16)
            sp.dma_start(w1raw[:, E, :], wfc_s).then_inc(shared_loaded, 16)
            sp.dma_start(w2raw[:, E], wproj_s.rearrange("(j p) c -> p j c", p=P)).then_inc(shared_loaded, 16)
            for g in range(NB):
                sp.wait_ge(x_loaded[g], 16)
            sp.wait_ge(shared_loaded, 32)
            sp.dma_start(w1raw[:, 0:E], wfc.rearrange("e c h -> c e h")).then_inc(routed_loaded, 16)
            sp.dma_start(w2raw[:, 0:E], wproj.rearrange("e (j p) c -> p e j c", p=P)).then_inc(routed_loaded, 16)
            for layer in range(LAYERS):
                with sp.Fori(0, NB) as g:
                    sp.wait_ge(xsplit_ready, layer * NB + g + 1)
                    sp.dma_start(xsplit_dram[layer][ds(g * T_SEQ, T_SEQ), :].rearrange("(t p) c -> p t c", p=P),
                                 xsplit[:, ds(g * TG, TG)].rearrange("p t s c -> p t (s c)")).then_inc(xsplit_stored, 16)
                if layer == 0:
                    sp.wait_ge(b1_parts_ready, 1)
                    for s in range(3):
                        sp.dma_start(b1_flat[s:s + 1, :].rearrange("a (q c) -> a q c", c=P),
                                     b1_parts[:, s, :]).then_inc(b1_flat_ready, 16)
                for k in range(U):
                    sp.wait_ge(scattered[k], 16 * BODIES * (layer + 1))
                for g in range(NB):
                    for k in range(K):
                        sp.dma_start(routed[:, k * N + g * T_SEQ:k * N + (g + 1) * T_SEQ].rearrange(
                                         "p (t c) -> p t c", c=C),
                                     routed_dram[layer][k * N + g * T_SEQ:k * N + (g + 1) * T_SEQ, :].rearrange(
                                         "(t p) c -> p t c", p=P)).then_inc(routed_back[g], 16)
            with sp.Fori(0, NB) as g:
                sp.wait_ge(x_done, g + 1)
                sp.dma_start(out_rows[:, ds(g * TG, TG), :],
                             xs[:, ds(g * T_SEQ, T_SEQ)].rearrange("p (t c) -> p t c", c=C)).then_inc(out_stored, 16)
            sp.wait_ge(out_stored, 16 * NB)
            sp.wait_ge(xsplit_stored, 16 * NB * LAYERS)

        @block.gpsimd
        def _(pool):
            steps = Steps(pool, pool_step)
            pool.memset(ident[:, :], 0.0)
            pool.memset(before[:, :], 1.0)
            pool.memset(ones16[:, :], 1.0)
            pool.memset(ones_row[:, :], 1.0)
            pool.memset(ones8[:, :], 1.0)
            pool.memset(ones_bf[:, :], 1.0)
            pool.memset(carry[:, :], 1.0)
            pool.memset(minus_half[:, :, :], -0.5)
            pool.memset(peak[:, :], 0.0)
            pool.memset(gates[:, :, E:E + 1], 0.5)
            pool.iota(rank8[:, :], [[-1, E]], base=E, channel_multiplier=0, allow_small_or_imprecise_dtypes=True)
            pool.iota(lane[:, :], [[1, P]], base=0, channel_multiplier=0, allow_small_or_imprecise_dtypes=True)
            pool.iota(slot_tile[:, :], [[1, G]], base=0, channel_multiplier=0, allow_small_or_imprecise_dtypes=True)
            pool.iota(pair_no[:, :], [[1, NC]], base=1, channel_multiplier=0, allow_small_or_imprecise_dtypes=True)
            pool.iota(own_lane[:, :], [[0, 1]], base=0, channel_multiplier=1, allow_small_or_imprecise_dtypes=True)
            steps.link(pool.iota(spare_row[:, :], [[P, G]], base=KN + P, channel_multiplier=1,
                                 allow_small_or_imprecise_dtypes=True))
            pool.memset(carry[:, :].rearrange("p (e t) -> p e t", e=E)[:, :, 0:1], 0.0)
            pool.affine_select(out=before[:, :], in_=before[:, :], compare_op=ALU.is_gt, fill=0.0, base=0,
                               pattern=[[1, P]], channel_multiplier=-1)
            steps.link(pool.affine_select(out=ident[:, :], in_=ident[:, :], compare_op=ALU.not_equal, fill=1.0,
                                          base=0, pattern=[[-1, P]], channel_multiplier=1))
            pool.tensor_copy(ident16[:, :], ident[:, :]).then_inc(consts_made, 1)

            def ln_rstd(layer, g):
                at = slice(g * TG, (g + 1) * TG)
                pool.wait_ge(var_ready, layer * NB + g + 1)
                steps.link(pool.tensor_scalar(veps[:, at], moments[:, at, 1], EPS, X_SCALE ** -2.0, ALU.add, ALU.mult))
                pool.tensor_tensor(rstd[:, at], veps[:, at], minus_half[:, 0], ALU.pow).then_inc(rstd_ready, 1)

            def att_rstd(g):
                at = slice(g * TG, (g + 1) * TG)
                pool.wait_ge(att_var_ready, g + 1)
                pool.tensor_tensor(att_r[:, :, at], att_q[:, :, at], minus_half[:, :, :], ALU.pow
                                   ).then_inc(att_rstd_ready, 1)

            for g in range(NB):
                ln_rstd(0, g)

            for layer in range(LAYERS):
                for g in range(NB):
                    at = slice(g * T_SEQ, (g + 1) * T_SEQ)
                    pool.wait_ge(bias_moved, layer * NB + g + 1)
                    pool.tensor_tensor(xs[:, at], xs[:, at], xn[:, at], ALU.add).then_inc(bias_added, 1)
                pool.wait_ge(rows_ready, layer + 1)
                pool.wait_ge(xsplit_stored, 16 * NB * (layer + 1))

                def gather(i):
                    k, n = i % U, i // U
                    if layer * BODIES + n:
                        pool.wait_ge(gathered[k], 16 * (layer * BODIES + n))
                    pool.indirect_dma_start(
                        out=xg[:, i * 2 * C:(i + 1) * 2 * C], out_offset=None, in_=xsplit_dram[layer][:, :],
                        in_offset=bass.IndirectOffsetOnAxis(ap=gather_row[:, i:i + 1], axis=0),
                    ).then_inc(gathered[k], 16)

                for i in range(AHEAD):
                    gather(i)
                for i in range(G):
                    pool.wait_ge(y_ready, layer * G + i + 1)
                    pool.indirect_dma_start(
                        out=routed_dram[layer][:, :],
                        out_offset=bass.IndirectOffsetOnAxis(ap=scatter_row[:, i:i + 1], axis=0),
                        in_=y[:, i % U, :], in_offset=None,
                    ).then_inc(scattered[i % U], 16)
                    if i + AHEAD < G:
                        gather(i + AHEAD)
                if layer == 0:
                    for s in range(NB + 2):
                        if 1 <= s <= NB:
                            at = slice((s - 1) * T_SEQ, s * T_SEQ)
                            pool.wait_ge(xatt_ready, s)
                            pool.tensor_tensor(xs[:, at], xs[:, at], xatt[:, at], ALU.add).then_inc(x_sum_ready, 1)
                        if s < NB:
                            att_rstd(s)
                        if s >= 2:
                            ln_rstd(1, s - 2)

        @block.scalar
        def _(act):
            small = [(wr_raw[:, :], wr), (b1rows[0:E * J, :], bfc.rearrange("e (j p) -> (e j) p", p=P)),
                     (b1rows[E * J:, :], bfc_s.rearrange("(j p) -> j p", p=P)), (b2rows[0:E, :], bproj),
                     (b2rows[E:E + 1, :], bproj_s.rearrange("(a c) -> a c", a=1)),
                     (w_att_raw[:, 0], wg), (w_att_raw[:, 1], wc)]
            small += [(cols[:, n:n + 1], v.rearrange("(p a) -> p a", a=1)) for n, v in enumerate((gamma, beta, bg))]
            assert len(small) == SMALL
            for dst, src in small:
                act.dma_start(dst, src).then_inc(small_loaded, 16)
            act.dma_start(cols[:, 3:4], bc.rearrange("(p a) -> p a", a=1)).then_inc(small_loaded, 16)
            act.preload_act_table(ACT.Gelu_apprx_tanh)

            def ln_hi(layer, g):
                act.wait_ge(ln_ready, layer * NB + g + 1)
                act.copy(xsplit[:, g * TG:(g + 1) * TG, 0, :],
                         xn[:, g * T_SEQ:(g + 1) * T_SEQ].rearrange("p (t c) -> p t c", c=C)).then_inc(ln_high, 1)

            def move_xT(layer, g):
                act.wait_ge(xT_turned, layer * NB + g + 1)
                act.copy(xT32[:, :, g * (T_SEQ // 2):(g + 1) * (T_SEQ // 2)],
                         bank(4 + g % 2).rearrange("p (s t) -> p s t", s=2)).then_inc(xT_ready, 1)

            for g in range(NB):
                ln_hi(0, g)
                if g:
                    move_xT(0, g - 1)
            move_xT(0, NB - 1)

            for layer in range(LAYERS):
                act.wait_ge(gap_ready, layer + 1)
                act.activation(gap_tanh[:, :], gap[:, :], ACT.Tanh, scale=un[:, 5:6]).then_inc(gap_tanh_ready, 1)
                for g in range(NB):
                    act.wait_ge(gates_turned, layer * NB + g + 1)
                    act.copy(gatesT[:, g * T_SEQ:(g + 1) * T_SEQ], bank(g)[0:E + 1, :]).then_inc(gatesT_ready, 1)
                for g in range(NB):
                    act.wait_ge(bias_ready, layer * NB + g + 1)
                    act.copy(xn[:, g * T_SEQ:(g + 1) * T_SEQ], bank(g)).then_inc(bias_moved, 1)
                if layer == 0:
                    act.wait_ge(scales_ready, 2)
                    act.activation(w1[:, 0:E, 0, :], w1raw[:, 0:E], ACT.Identity,
                                   scale=scale_w[:, 4:5]).then_inc(weights_hi, 1)
                    act.activation(w2[:, 0:E, :, 0, :], w2raw[:, 0:E], ACT.Identity,
                                   scale=scale_w[:, 5:6]).then_inc(weights_hi, 1)

                def sh_act(g, j):
                    act.wait_ge(sh_up, layer * NB * J + g * J + j + 1)
                    act.activation(h_sh[:, j, :], bank(j), ACT.Gelu_apprx_tanh, scale=un[:, 0:1],
                                   bias=b1T[:, E * J + j:E * J + j + 1]).then_inc(sh_gelu, 1)

                def sh_hi(g, j):
                    act.wait_ge(sh_gelu, layer * NB * J + g * J + j + 1)
                    act.activation(hs_sh[:, 0, j, :], h_sh[:, j, :], ACT.Identity,
                                   scale=scale_w[:, 2:3]).then_inc(sh_high, 1)

                with act.Fori(0, NB) as g:
                    sh_act(g, 0)
                    for j in range(J):
                        if j + 1 < J:
                            sh_act(g, j + 1)
                        if j < J - layer:
                            sh_hi(g, j)

                def gelu(i, par):
                    act.wait_ge(up_ready, layer * G + i + 1)
                    act.activation(h[:, par, :], bank(par), ACT.Gelu_apprx_tanh,
                                   scale=un[:, 2:3]).then_inc(gelu_ready, 1)

                def high(i, par):
                    act.wait_ge(h_slots_turned, layer * G + i + 1)
                    act.activation(hs[:, par, 0, :], bank(2 + par), ACT.Identity,
                                   scale=scale_w[:, 6:7]).then_inc(high_ready, 1)

                def move_low(i, par):
                    act.wait_ge(down_ready, layer * G + i + 1)
                    act.copy(y_low[:, par, :], bank(4 + par)[:, C:2 * C]).then_inc(y_low_ready, 1)

                gelu(0, 0)
                gelu(1, 1)
                high(0, 0)
                with act.Fori(0, BODIES - 1) as n:
                    for k in range(U):
                        gelu(n * U + k + 2, k % 2)
                        high(n * U + k + 1, (k + 1) % 2)
                        move_low(n * U + k, k % 2)
                for i in range(G - U, G):
                    if i + 2 < G:
                        gelu(i + 2, i % 2)
                    if i + 1 < G:
                        high(i + 1, (i + 1) % 2)
                    move_low(i, i % 2)

                if layer == 0:
                    for s in range(1, NB + 4):
                        b, par = s - 1, (s - 1) % 2
                        if s <= NB:
                            act.wait_ge(xatt_ready, b + 1)
                            act.wait_ge(att_rstd_ready, b + 1)
                            for t in range(b * TG, (b + 1) * TG):
                                ins = act.activation(xn[:, t * C:(t + 1) * C], xatt[:, t * C:(t + 1) * C],
                                                     ACT.Identity, scale=att_r[:, 1, t:t + 1])
                            ins.then_inc(norm_ready, 1)
                        if s >= 4:
                            move_xT(1, s - 4)
                        if s <= NB:
                            act.wait_ge(norm_turned, b + 1)
                            act.activation(normT[:, par], bank(0), ACT.Identity, scale=cols[:, 0:1],
                                           bias=cols[:, 1:2]).then_inc(normT_ready, 1)
                            act.wait_ge(gates_in, b + 1)
                            if b >= 2:
                                act.wait_ge(hT_ready, b - 1)
                            act.activation(zh[:, par], bank(1), ACT.Tanh, scale=0.5,
                                           bias=half_bg[:, 0:1]).then_inc(tanh_ready, 1)
                            act.wait_ge(tanh_ready, b + 1)
                            act.activation(zt[:, par], zh[:, par], ACT.Copy, scale=0.5, bias=0.5)
                            act.activation(at_[:, par], zh[:, par], ACT.Copy, scale=-0.5,
                                           bias=0.5).then_inc(z_ready, 1)
                        if 3 <= s < NB + 3:
                            ln_hi(1, s - 3)

        @block.vector
        def _(dve):
            steps = Steps(dve, dve_step)
            link = steps.link
            def add_stats(g):
                for t in range(g * TG, (g + 1) * TG):
                    ins = dve.bn_stats(bn[:, t, :], xs[:, t * C:(t + 1) * C])
                link(ins)
                for t in range(g * TG, (g + 1) * TG):
                    ins = dve.bn_aggr(moments[:, t, :], bn[:, t, :])
                return ins

            def normalize(dst, factor, g):
                for t in range(g * TG, (g + 1) * TG):
                    ins = dve.tensor_scalar(dst[:, t * C:(t + 1) * C], xs[:, t * C:(t + 1) * C], moments[:, t, 0:1],
                                            factor[:, t:t + 1], ALU.subtract, ALU.mult)
                return ins

            def ln_norm(layer, g):
                dve.wait_ge(rstd_ready, layer * NB + g + 1)
                normalize(xn, rstd, g).then_inc(ln_ready, 1)

            def ln_low(layer, g):
                dve.wait_ge(ln_high, layer * NB + g + 1)
                dve.tensor_tensor(xsplit[:, g * TG:(g + 1) * TG, 1, :],
                                  xn[:, g * T_SEQ:(g + 1) * T_SEQ].rearrange("p (t c) -> p t c", c=C),
                                  xsplit[:, g * TG:(g + 1) * TG, 0, :], ALU.subtract).then_inc(xsplit_ready, 1)

            def spread_peaks(n, first, rnd):
                dve.wait_ge(peaksT_ready, rnd)
                link(dve.tensor_reduce(peak_max[0:n, :], bank(7)[0:n, 0:P], AX.X, ALU.max))
                dve.tensor_scalar(peak_diag[0:n, 0:n], ident[0:n, 0:n], peak_max[0:n, 0:1], None,
                                  ALU.mult).then_inc(peak_diag_ready, 1)
                dve.wait_ge(peaks_spread, rnd)
                link(dve.tensor_copy(peak_all[:, first:first + n], bank(7, n)))

            def power_of_two(dst, src):
                link(dve.tensor_scalar(dst.bitcast(I32), src.bitcast(I32), 0x7F800000, None, ALU.bitwise_and))
                link(dve.tensor_scalar(dst, dst, TINY, None, ALU.max))

            def scales(w1_, w2_, b1_, s_w, s_h, u_up, u_down):
                link(dve.scalar_tensor_tensor(pow2[:, 7:8], peak_all[:, w1_:w1_ + 1], float(P),
                                              peak_all[:, b1_:b1_ + 1], ALU.mult, ALU.add))
                power_of_two(pow2[:, 2:3], pow2[:, 7:8])
                power_of_two(pow2[:, 0:1], peak_all[:, w1_:w1_ + 1])
                power_of_two(pow2[:, 1:2], peak_all[:, w2_:w2_ + 1])
                link(dve.reciprocal(inv[:, 0:3], pow2[:, 0:3]))
                dve.tensor_scalar(scale_w[:, s_w:s_w + 2], inv[:, 0:2], TOP, None, ALU.mult)
                dve.tensor_scalar(scale_w[:, s_h:s_h + 1], inv[:, 2:3], TOP, None, ALU.mult)
                dve.tensor_scalar(un[:, u_up:u_up + 1], pow2[:, 0:1], 1.0 / (TOP * X_SCALE), None, ALU.mult)
                link(dve.scalar_tensor_tensor(un[:, u_down:u_down + 1], pow2[:, 2:3], TOP ** -2.0, pow2[:, 1:2],
                                              ALU.mult, ALU.mult))

            def first_scales():
                dve.wait_ge(shared_loaded, 32)
                dve.wait_ge(small_loaded, 16 * (SMALL + 1))
                dve.tensor_reduce(peak[:, 0:1], w1raw[:, E], AX.X, ALU.max, apply_absolute_value=True)
                dve.tensor_reduce(peak[:, 1:2], w2raw[:, E].rearrange("p j c -> p (j c)"), AX.X, ALU.max,
                                  apply_absolute_value=True)
                dve.tensor_reduce(peak[:, 2:3], wr_raw[:, :], AX.X, ALU.max, apply_absolute_value=True)
                dve.tensor_reduce(peak[0:(E + 1) * J, 3:4], b1rows[:, :], AX.X, ALU.max,
                                  apply_absolute_value=True).then_inc(peaks_ready, 1)
                spread_peaks(4, 0, 1)
                scales(0, 1, 3, 0, 2, 0, 1)
                power_of_two(pow2[:, 3:4], peak_all[:, 2:3])
                link(dve.reciprocal(inv[:, 3:4], pow2[:, 3:4]))
                dve.tensor_scalar(un[:, 4:5], un[:, 1:2], 0.5, None, ALU.mult)
                dve.tensor_scalar(un[:, 5:6], pow2[:, 3:4], 0.5 / (TOP * X_SCALE), None, ALU.mult)
                link(dve.tensor_scalar(scale_w[:, 3:4], inv[:, 3:4], TOP, None, ALU.mult))
                link(dve.tensor_scalar(wr16[:, 0, :], wr_raw[:, :], scale_w[:, 3:4], None, ALU.mult))
                dve.scalar_tensor_tensor(wr16[:, 1, :], wr_raw[:, :], scale_w[:, 3:4], wr16[:, 0, :], ALU.mult,
                                         ALU.subtract).then_inc(router_w_ready, 1)
                dve.tensor_scalar(half_bg[:, :], cols[:, 2:3], 0.5, None, ALU.mult)
                dve.wait_ge(att_w_turned, 1)
                dve.tensor_copy(b1T[:, :], bank(0, (E + 1) * J))
                link(dve.tensor_copy(w_att[:, :, :].rearrange("p k c -> p (k c)"), bank(1, 2 * C)))

            def split_shared():
                for raw, hi, lo, col in ((w1raw[:, E], w1[:, E, 0], w1[:, E, 1], 0),
                                         (w2raw[:, E], w2[:, E, :, 0], w2[:, E, :, 1], 1)):
                    link(dve.tensor_scalar(hi, raw, scale_w[:, col:col + 1], None, ALU.mult))
                    ins = dve.scalar_tensor_tensor(lo, raw, scale_w[:, col:col + 1], hi, ALU.mult, ALU.subtract)
                ins.then_inc(weights_split, 1)

            def routed_scales():
                spread_peaks(2, 4, 2)
                scales(4, 5, 3, 4, 6, 2, 3)
                dve.tensor_copy(pow2[:, 6:7], pow2[:, 7:8]).then_inc(scales_ready, 2)
                link(dve.tensor_scalar(b1_rest[:, :], b1rows[0:E * J, :], scale_w[0:E * J, 4:5], X_SCALE, ALU.mult,
                                       ALU.mult))
                for s in range(3):
                    ins = dve.tensor_copy(b1_parts[:, s, :], b1_rest[:, :])
                    if s < 2:
                        link(ins)
                        link(dve.tensor_tensor(b1_rest[:, :], b1_rest[:, :], b1_parts[:, s, :], ALU.subtract))
                ins.then_inc(b1_parts_ready, 1)

            def choose(k, src):
                v = [pick[:, n, :].rearrange("p (t e) -> p t e", e=E) for n in range(2)]
                ranks = rank8[:, :].unsqueeze(1).broadcast_to([P, NT, E])
                link(dve.tensor_reduce(best[:, k, :], src, AX.X, ALU.max))
                link(dve.tensor_tensor(v[0], src, best[:, k, :].unsqueeze(2).broadcast_to([P, NT, E]), ALU.is_equal))
                link(dve.tensor_tensor(v[1], v[0], ranks, ALU.mult))
                link(dve.tensor_reduce(top_rank[:, :], v[1], AX.X, ALU.max))
                link(dve.tensor_tensor(chosen[:, k], ranks, top_rank[:, :].unsqueeze(2).broadcast_to([P, NT, E]),
                                       ALU.is_equal))

            def route(layer):
                dve.wait_ge(logits_ready, NB * (layer + 1))
                link(dve.tensor_reduce(logits[:, :, :],
                                       bank(7, NT * 2 * E).rearrange("p (t s e) -> p t e s", s=2, e=E),
                                       AX.X, ALU.add))
                choose(0, logits[:, :, :])
                link(dve.scalar_tensor_tensor(logits2[:, :, :], chosen[:, 0], -BIG, logits[:, :, :], ALU.mult,
                                              ALU.add))
                choose(1, logits2[:, :, :])
                dve.tensor_tensor(gap[:, :], best[:, 1, :], best[:, 0, :], ALU.subtract).then_inc(gap_ready, 1)
                link(dve.tensor_tensor(used[:, :].rearrange("p (e t) -> p t e", e=E), chosen[:, 0], chosen[:, 1],
                                       ALU.add))
                link(dve.tensor_tensor_scan(upto[:, :], carry[:, :], used[:, :], 0.0, ALU.mult, ALU.add))
                dve.tensor_copy(total[:, :].unsqueeze(2), upto[:, :].rearrange("p (e t) -> p e t", e=E)[:, :, NT - 1:NT])
                dve.tensor_tensor(ahead[:, :], upto[:, :], used[:, :], ALU.subtract).then_inc(used_ready, 1)
                make_gates(layer)
                dve.wait_ge(rank_ready, layer + 1)
                link(dve.tensor_scalar(tiles_i[:, 0, :], bank(6)[:, P:P + E], float(P - 1), None, ALU.add))
                link(dve.tensor_scalar(tiles_i[:, 1, :], tiles_i[:, 0, :], 7, None, ALU.logical_shift_right))
                link(dve.tensor_copy(tiles[:, :], tiles_i[:, 1, :]))
                link(dve.tensor_tensor_scan(tile_end[:, :], ones8[:, :], tiles[:, :], 0.0, ALU.mult, ALU.add))
                link(dve.tensor_tensor(tile_start[:, :], tile_end[:, :], tiles[:, :], ALU.subtract))
                link(dve.scalar_tensor_tensor(slot_of[:, :].rearrange("p (e t) -> p e t", e=E),
                                              tile_start[:, :].unsqueeze(2).broadcast_to([P, E, NT]), float(P),
                                              bank(6, P).rearrange("p (e t) -> p e t", e=E), ALU.mult, ALU.add))
                sk = [slot_k[:, k, :].rearrange("p (t e) -> p t e", e=E) for k in range(K)]
                for k in range(K):
                    ins = dve.tensor_tensor(sk[k], chosen[:, k], slot_of[:, :].rearrange("p (e t) -> p t e", e=E),
                                            ALU.mult)
                link(ins)
                for k in range(K):
                    ins = dve.tensor_reduce(slot[:, k * NT:(k + 1) * NT], sk[k], AX.X, ALU.add)
                link(ins)
                link(dve.tensor_copy(slot_i[:, 0, :], slot[:, :]))
                dve.tensor_scalar(slot_i[:, 1, :], slot_i[:, 0, :], 7, None, ALU.logical_shift_right)
                link(dve.tensor_scalar(slot_i[:, 2, :], slot_i[:, 0, :], P - 1, None, ALU.bitwise_and))
                dve.tensor_copy(slot_g[:, :], slot_i[:, 1, :])
                link(dve.tensor_copy(slot_p[:, :], slot_i[:, 2, :]))
                link(dve.tensor_tensor(in_tile[:, :, :], slot_tile[:, :].unsqueeze(1).broadcast_to([P, NC, G]),
                                       slot_g[:, :].unsqueeze(2).broadcast_to([P, NC, G]), ALU.is_equal))
                dve.tensor_tensor(in_tile_id[:, :, 0, :], in_tile[:, :, :],
                                  pair_no[:, :].unsqueeze(2).broadcast_to([P, NC, G]), ALU.mult)
                dve.tensor_scalar(in_tile_id[:, :, 1, :], in_tile[:, :, :], own_lane[:, 0:1], None, ALU.mult)
                dve.tensor_tensor(in_lane[:, :, :], lane[:, :].unsqueeze(1).broadcast_to([P, NC, P]),
                                  slot_p[:, :].unsqueeze(2).broadcast_to([P, NC, P]), ALU.is_equal
                                  ).then_inc(onehots_ready, 1)
                link(dve.tensor_tensor(ended[:, :, :], slot_tile[:, :].unsqueeze(2).broadcast_to([P, G, E]),
                                       tile_end[:, :].unsqueeze(1).broadcast_to([P, G, E]), ALU.is_ge))
                link(dve.tensor_reduce(rt[:, 4, :], ended[:, :, :], AX.X, ALU.add))
                dve.tensor_scalar(tile_expert[:, :], rt[:, 4, :], float(E - 1), None, ALU.min
                                  ).then_inc(experts_ready, 1)
                if layer == 0:
                    routed_scales()
                    split_shared()
                dve.wait_ge(held_ready, layer + 1)
                link(dve.tensor_copy(held[:, :, :].rearrange("p s g -> p (s g)"), bank(6, 2 * G)))
                link(dve.scalar_tensor_tensor(row_id[:, :], held[:, 0, :], float(P), held[:, 1, :], ALU.mult, ALU.add))
                link(dve.tensor_scalar(rt[:, 0, :], row_id[:, :], -float(P), None, ALU.add))
                dve.tensor_scalar(rt[:, 1, :], rt[:, 0, :], float(N), -float(N), ALU.is_ge, ALU.mult)
                link(dve.scalar_tensor_tensor(rt[:, 2, :], rt[:, 0, :], 0.0, spare_row[:, :], ALU.is_lt, ALU.mult))
                dve.tensor_tensor(scatter_row[:, :], rt[:, 0, :], rt[:, 2, :], ALU.add)
                link(dve.tensor_tensor(rt[:, 3, :], rt[:, 0, :], rt[:, 1, :], ALU.add))
                dve.tensor_scalar(gather_row[:, :], rt[:, 3, :], 0.0, None, ALU.max).then_inc(rows_ready, 1)

            def make_gates(layer):
                dve.wait_ge(gap_tanh_ready, layer + 1)
                dve.tensor_scalar(gate[:, 0, :], gap_tanh[:, :], -0.25, 0.25, ALU.mult, ALU.add)
                link(dve.tensor_scalar(gate[:, 1, :], gap_tanh[:, :], 0.25, 0.25, ALU.mult, ALU.add))
                for k in range(K):
                    ins = dve.tensor_tensor(gates_k[:, k], chosen[:, k],
                                            gate[:, k, :].unsqueeze(2).broadcast_to([P, NT, E]), ALU.mult)
                link(ins)
                dve.tensor_tensor(gates[:, :, 0:E], gates_k[:, 0], gates_k[:, 1], ALU.add).then_inc(gates_ready, 1)

            def shared(layer):
                def sh_lo(g, j):
                    if layer and j == J - 1:
                        dve.wait_ge(sh_gelu, layer * NB * J + g * J + j + 1)
                        link(dve.tensor_scalar(hs_sh[:, 0, j, :], h_sh[:, j, :], scale_w[:, 2:3], None, ALU.mult))
                    else:
                        dve.wait_ge(sh_high, layer * NB * J + g * (J - layer) + j + 1)
                    dve.scalar_tensor_tensor(hs_sh[:, 1, j, :], h_sh[:, j, :], scale_w[:, 2:3], hs_sh[:, 0, j, :],
                                             ALU.mult, ALU.subtract).then_inc(sh_split, 1)

                def sh_add(g):
                    at = slice(g * T_SEQ, (g + 1) * T_SEQ)
                    dve.wait_ge(bias_added, layer * NB + g + 1)
                    dve.wait_ge(sh_down, layer * NB + g + 1)
                    return dve.scalar_tensor_tensor(xs[:, at], bank(4 + g % 2), un[:, 4:5], xs[:, at], ALU.mult,
                                                    ALU.add)

                def low_weights(which, g):
                    e = slice(g * E // NB, (g + 1) * E // NB)
                    dve.wait_ge(weights_hi, which + 1)
                    if which == 0:
                        return dve.scalar_tensor_tensor(w1[:, e, 1, :], w1raw[:, e], scale_w[:, 4:5], w1[:, e, 0, :],
                                                        ALU.mult, ALU.subtract)
                    return dve.scalar_tensor_tensor(w2[:, e, :, 1, :], w2raw[:, e], scale_w[:, 5:6], w2[:, e, :, 0, :],
                                                    ALU.mult, ALU.subtract)

                for g in range(NB):
                    for j in range(J):
                        sh_lo(g, j)
                        if g and j == 1:
                            sh_add(g - 1)
                        if layer == 0 and j % 2:
                            ins = low_weights(j // 2, g)
                if layer == 0:
                    ins.then_inc(weights_low, 1)
                sh_add(NB - 1)

            def routed_tiles(layer):
                def move_xg(i, par):
                    dve.wait_ge(xg_turned, layer * G + i + 1)
                    dve.tensor_copy(xgT[:, par, :], bank(6 + par, P).bitcast(F16)).then_inc(xgT_ready, 1)

                def low(i, par):
                    dve.wait_ge(high_ready, layer * G + i + 1)
                    dve.scalar_tensor_tensor(hs[:, par, 1, :], bank(2 + par), scale_w[:, 6:7], hs[:, par, 0, :],
                                             ALU.mult, ALU.subtract).then_inc(split_ready, 1)

                def sum_y(i, k, sent):
                    if sent is not None:
                        dve.wait_ge(scattered[k], 16 * sent)
                    dve.wait_ge(y_low_ready, layer * G + i + 1)
                    dve.tensor_tensor(y[:, k, :], bank(4 + k % 2, C), y_low[:, k % 2, :], ALU.add).then_inc(y_ready, 1)

                def body(n, sent):
                    for k in range(U):
                        i = n * U + k
                        if not isinstance(n, int) or i + 3 < G:
                            move_xg(i + 3, (k + 1) % 2)
                        if not isinstance(n, int) or i + 1 < G:
                            low(i + 1, (k + 1) % 2)
                        sum_y(i, k, sent)

                for i in range(3):
                    move_xg(i, i % 2)
                low(0, 0)
                body(0, layer * BODIES if layer else None)
                with dve.Fori(1, BODIES - 1) as n:
                    body(n, layer * BODIES + n)
                body(BODIES - 1, layer * BODIES + BODIES - 1)

            def combine(layer, g):
                dve.wait_ge(routed_back[g], 16 * K * (layer + 1))
                for k in range(K):
                    for t in range(g * TG, (g + 1) * TG):
                        at = slice(t * C, (t + 1) * C)
                        ins = dve.scalar_tensor_tensor(xs[:, at], routed[:, k * N + t * C:k * N + (t + 1) * C],
                                                       gate_un[:, k, t:t + 1], xs[:, at], ALU.mult, ALU.add)
                    if k == 0:
                        link(ins)
                return ins

            def att_stats(g):
                at = slice(g * TG, (g + 1) * TG)
                link(add_stats(g))
                dve.tensor_scalar(att_q[:, 0, at], moments[:, at, 1], EPS, None, ALU.add)
                link(dve.tensor_scalar(att_v[:, 0, at], moments[:, at, 1], EPS, None, ALU.add))
                link(dve.reciprocal(att_v[:, 1, at], att_v[:, 0, at]))
                link(dve.tensor_tensor(att_v[:, 2, at], moments[:, at, 1], att_v[:, 1, at], ALU.mult))
                dve.tensor_scalar(att_q[:, 1, at], att_v[:, 2, at], EPS, None, ALU.add).then_inc(att_var_ready, 1)

            def gru():
                for s in range(NB + 4):
                    if 1 <= s <= NB:
                        dve.wait_ge(att_rstd_ready, s)
                        normalize(xatt, att_r[:, 0], s - 1).then_inc(xatt_ready, 1)
                    if 2 <= s < NB + 2:
                        b, par = s - 2, s % 2
                        dve.wait_ge(cand_in, b + 1)
                        dve.wait_ge(z_ready, b + 1)
                        if b >= 2:
                            dve.wait_ge(h_turned, b - 1)
                        link(dve.scalar_tensor_tensor(bt[:, par], bank(2), cols[:, 3:4], zt[:, par],
                                                      ALU.add, ALU.mult))
                        dve.tensor_tensor_scan(ht[:, par], at_[:, par], bt[:, par], 0.0, ALU.mult,
                                               ALU.add).then_inc(hT_ready, 1)
                    if s < NB:
                        link(combine(0, s))
                        att_stats(s)
                    if 3 <= s < NB + 3:
                        ln_norm(1, s - 3)
                    if 2 <= s < NB + 2:
                        b = s - 2
                        dve.wait_ge(h_turned, b + 1)
                        dve.wait_ge(x_sum_ready, b + 1)
                        link(dve.tensor_tensor(xs[:, b * T_SEQ:(b + 1) * T_SEQ], bank(3),
                                               xs[:, b * T_SEQ:(b + 1) * T_SEQ], ALU.add))
                        add_stats(b).then_inc(var_ready, 1)
                    if 3 <= s < NB + 3:
                        ln_low(1, s - 3)

            def routed_peaks():
                dve.wait_ge(routed_loaded, 32)
                dve.tensor_reduce(peak[:, 4:5], w1raw[:, 0:E].rearrange("p e h -> p (e h)"), AX.X, ALU.max,
                                  apply_absolute_value=True)
                dve.tensor_reduce(peak[:, 5:6], w2raw[:, 0:E].rearrange("p e j c -> p (e j c)"), AX.X, ALU.max,
                                  apply_absolute_value=True).then_inc(peaks_ready, 1)

            dve.wait_ge(consts_made, 1)
            for g in range(NB):
                dve.wait_ge(x_loaded[g], 16)
                add_stats(g).then_inc(var_ready, 1)
            for g in range(NB):
                ln_norm(0, g)
                if g:
                    ln_low(0, g - 1)
            ln_low(0, NB - 1)
            first_scales()
            routed_peaks()
            for layer in range(LAYERS):
                route(layer)
                link(dve.tensor_scalar(gate_un[:, :, :], gate[:, :, :], un[:, 3:4], None, ALU.mult))
                shared(layer)
                routed_tiles(layer)
                if layer == 0:
                    gru()
            for g in range(NB):
                combine(1, g).then_inc(x_done, 1)

        @block.tensor
        def _(pe):
            def transpose_peaks(n, first, rnd):
                pe.wait_ge(peaks_ready, rnd)
                pe.transpose(bank(7)[0:n, 0:P], peak[:, first:first + n], ident[:, :]).then_inc(peaksT_ready, 1)
                pe.wait_ge(peak_diag_ready, rnd)
                pe.matmul(bank(7, n), ones_row[0:n, :], peak_diag[0:n, 0:n], start=True,
                          stop=True).then_inc(peaks_spread, 1)

            def three(out, wh, wl, xh, xl, first, last):
                pe.matmul(out, wh, xh, start=first, stop=False, skip_group_check=True)
                pe.matmul(out, wh, xl, start=False, stop=False, skip_group_check=True)
                return pe.matmul(out, wl, xh, start=False, stop=last, skip_group_check=True)

            regs = [pe.alloc_register(f"expert_{k}") for k in range(U + 3)]
            pe.wait_ge(consts_made, 1)

            def prepare_weights():
                transpose_peaks(4, 0, 1)
                pe.wait_ge(small_loaded, 16 * (SMALL + 1))
                pe.transpose(bank(0, (E + 1) * J), b1rows[:, :], ident[0:(E + 1) * J, 0:(E + 1) * J])
                pe.transpose(bank(1)[:, 0:C], w_att_raw[:, 0], ident[:, :])
                pe.transpose(bank(1)[:, C:2 * C], w_att_raw[:, 1], ident[:, :]).then_inc(att_w_turned, 1)

            def turn_x(layer, g):
                pe.wait_ge(xsplit_ready, layer * NB + g + 1)
                if g >= 2:
                    pe.wait_ge(xT_ready, layer * NB + g - 1)
                for s in range(2):
                    for t in range(TG):
                        ins = pe.transpose(bank(4 + g % 2).bitcast(F16)[:, s * T_SEQ + t * P:s * T_SEQ + (t + 1) * P],
                                           xsplit[:, g * TG + t, s, :], ident16[:, :])
                ins.then_inc(xT_turned, 1)

            def router(layer, g):
                pe.wait_ge(xT_ready, layer * NB + g + 1)
                for t in range(g * TG, (g + 1) * TG):
                    at = slice(t * 2 * E, (t + 1) * 2 * E)
                    pe.matmul(bank(7)[:, at], xT[:, 0, t * P:(t + 1) * P], wr16[:, :, :].rearrange("p s e -> p (s e)"),
                              start=True, stop=False)
                    ins = pe.matmul(bank(7)[:, at], xT[:, 1, t * P:(t + 1) * P],
                                    wr16[:, :, :].rearrange("p s e -> p (s e)"), start=False, stop=True)
                ins.then_inc(logits_ready, 1)

            for g in range(NB):
                turn_x(0, g)
            prepare_weights()
            pe.wait_ge(router_w_ready, 1)
            for g in range(NB):
                router(0, g)

            for layer in range(LAYERS):
                pe.wait_ge(used_ready, layer + 1)
                pe.matmul(bank(6, P), before[:, :], used[:, :], start=True, stop=False)
                pe.matmul(bank(6, P), ones16[:, :], ahead[:, :], start=False, stop=True)
                pe.matmul(bank(6)[:, P:P + E], ones16[:, :], total[:, :], start=True, stop=True).then_inc(rank_ready, 1)
                pe.wait_ge(gates_ready, layer + 1)
                for t in range(NT):
                    ins = pe.transpose(bank(t // TG)[0:E + 1, (t % TG) * P:(t % TG + 1) * P], gates[:, t, :], ident[:, :])
                    if t % TG == TG - 1:
                        ins.then_inc(gates_turned, 1)
                for t in range(NT):
                    if t % TG == 0:
                        pe.wait_ge(gatesT_ready, layer * NB + t // TG + 1)
                    ins = pe.matmul(bank(t // TG)[:, (t % TG) * P:(t % TG + 1) * P], gatesT[:, t * P:(t + 1) * P],
                                    b2rows[:, :], start=True, stop=True)
                    if t % TG == TG - 1:
                        ins.then_inc(bias_ready, 1)
                if layer == 0:
                    transpose_peaks(2, 4, 2)
                pe.wait_ge(onehots_ready, layer + 1)
                for n in range(NC):
                    ins = pe.matmul(bank(6, 2 * G), in_lane[:, n, :], in_tile_id[:, n].rearrange("p s g -> p (s g)"),
                                    start=(n == 0), stop=(n == NC - 1))
                ins.then_inc(held_ready, 1)
                if layer == 0:
                    pe.wait_ge(weights_split, 1)

                def sh_first(g, j):
                    three(bank(j), w1[:, E, 0, j * P:(j + 1) * P], w1[:, E, 1, j * P:(j + 1) * P],
                          xT[:, 0, ds(g * T_SEQ, T_SEQ)], xT[:, 1, ds(g * T_SEQ, T_SEQ)], True, True
                          ).then_inc(sh_up, 1)

                def sh_second(g, j, out):
                    pe.wait_ge(sh_split, layer * NB * J + g * J + j + 1)
                    for t in range(TG):
                        hh, hl = (hs_sh[:, s, j, t * P:(t + 1) * P] for s in range(2))
                        ins = three(out[:, t * C:(t + 1) * C], hh, hl, w2[:, E, j, 0], w2[:, E, j, 1],
                                    j == 0 and t == 0, j == J - 1)
                    if j == J - 1:
                        ins.then_inc(sh_down, 1)

                pe.wait_ge(bias_moved, NB * (layer + 1))
                for j in range(J):
                    sh_first(0, j)
                for g in range(NB):
                    for j in range(J):
                        sh_second(g, j, bank(4 + g % 2))
                        if g + 1 < NB:
                            sh_first(g + 1, j)

                def turn(i, k, sent):
                    pe.wait_ge(gathered[k % U], 16 * (layer * BODIES + sent))
                    for s in range(2):
                        ins = pe.transpose(bank(6 + k % 2, P).bitcast(F16)[:, s * P:(s + 1) * P],
                                           xg[:, ds(i * 2 * C + s * C, C)], ident16[:, :])
                    ins.then_inc(xg_turned, 1)

                def up(i, par, e):
                    pe.wait_ge(xgT_ready, layer * G + i + 1)
                    wh, wl = (w1f[:, ds(e * (2 * HID) + s * HID, HID)] for s in range(2))
                    xh, xl = xgT[:, par, 0:P], xgT[:, par, P:2 * P]
                    pe.matmul(bank(par), xh, wh, start=True, stop=False)
                    pe.matmul(bank(par), xl, wh, start=False, stop=False)
                    pe.matmul(bank(par), xh, wl, start=False, stop=False)
                    pe.matmul(bank(par), ones_bf[:, :], b1_flat[:, ds(e * HID, HID)], start=False,
                              stop=True).then_inc(up_ready, 1)

                def turn_h(i, par):
                    pe.wait_ge(gelu_ready, layer * G + i + 1)
                    for j in range(J):
                        ins = pe.transpose(bank(2 + par)[:, j * P:(j + 1) * P], h[:, par, j * P:(j + 1) * P],
                                           ident[:, :])
                    ins.then_inc(h_slots_turned, 1)

                def down(i, par, e):
                    pe.wait_ge(split_ready, layer * G + i + 1)
                    for j in range(J):
                        hh, hl = (hs[:, par, s, j * P:(j + 1) * P] for s in range(2))
                        at = e * (2 * HID) + j * 2 * C
                        pe.matmul(bank(4 + par, 2 * C), hh, w2f[:, ds(at, 2 * C)], start=(j == 0), stop=False,
                                  skip_group_check=True)
                        ins = pe.matmul(bank(4 + par, C), hl, w2f[:, ds(at, C)], start=False, stop=(j == J - 1),
                                        skip_group_check=True)
                    ins.then_inc(down_ready, 1)

                def expert_regs(first, n, regs):
                    pe.load(regs[0:n], tile_expert[0:1, ds(first, n)])
                    return [pe.snap(r, min_val=0, max_val=E - 1) for r in regs[0:n]]

                pe.wait_ge(experts_ready, layer + 1)
                if layer == 0:
                    pe.wait_ge(b1_flat_ready, 16 * 3)
                    pe.wait_ge(weights_low, 1)
                e = expert_regs(0, 3, regs)
                turn(0, 0, 1)
                turn(1, 1, 1)
                up(0, 0, e[0])
                turn(2, 2, 1)
                up(1, 1, e[1])
                turn_h(0, 0)
                turn(3, 3, 1)
                up(2, 0, e[2])
                with pe.Fori(0, BODIES - 1) as n:
                    e = expert_regs(n * U, U + 3, regs)
                    for k in range(U):
                        turn_h(n * U + k + 1, (k + 1) % 2)
                        down(n * U + k, k % 2, e[k])
                        turn(n * U + k + 4, k, n + 2)
                        up(n * U + k + 3, (k + 1) % 2, e[k + 3])
                e = expert_regs(G - U, U, regs)
                for k in range(U):
                    i = G - U + k
                    if i + 1 < G:
                        turn_h(i + 1, (k + 1) % 2)
                    down(i, k % 2, e[k])
                    if i + 3 < G:
                        up(i + 3, (k + 1) % 2, e[k + 3])

                if layer == 0:
                    for s in range(1, NB + 4):
                        b, par = s - 1, (s - 1) % 2
                        if s >= 4:
                            turn_x(1, s - 4)
                        if s <= NB:
                            pe.wait_ge(norm_ready, b + 1)
                            for t in range(TG):
                                ins = pe.transpose(bank(0)[:, t * P:(t + 1) * P],
                                                   xn[:, b * T_SEQ + t * C:b * T_SEQ + (t + 1) * C], ident[:, :])
                            ins.then_inc(norm_turned, 1)
                        if s >= 4:
                            router(1, s - 4)
                        if s <= NB:
                            pe.wait_ge(normT_ready, b + 1)
                            if b:
                                pe.wait_ge(hT_ready, b)
                            pe.matmul(bank(1), w_att[:, 0], normT[:, par], start=True, stop=True).then_inc(gates_in, 1)
                            pe.matmul(bank(2), w_att[:, 1], normT[:, par], start=True, stop=True).then_inc(cand_in, 1)
                        if 2 <= s < NB + 2:
                            b, par = s - 2, s % 2
                            pe.wait_ge(hT_ready, b + 1)
                            if b:
                                pe.wait_ge(var_ready, NB + b)
                            for t in range(TG):
                                ins = pe.transpose(bank(3)[:, t * P:(t + 1) * P], ht[:, par, t * P:(t + 1) * P],
                                                   ident[:, :])
                            ins.then_inc(h_turned, 1)


_INS = ["L0_attn_x", "L0_attn_gamma", "L0_attn_beta", "L0_attn_Wg", "L0_attn_bg", "L0_attn_Wc", "L0_attn_bc",
        "L0_ffn_Wfc_s", "L0_ffn_bfc_s", "L0_ffn_Wproj_s", "L0_ffn_bproj_s", "L0_ffn_Wr", "L0_ffn_Wfc", "L0_ffn_bfc",
        "L0_ffn_Wproj", "L0_ffn_bproj"]


def kernel(**inputs):
    import numpy as np
    import concourse.bacc as bacc
    from concourse.bass_utils import run_bass_kernel_spmd

    nc = bacc.Bacc("TRN2", target_bir_lowering=False, num_devices=1)
    arrays, args = {}, []
    for name in _INS:
        a = np.ascontiguousarray(inputs[name])
        arrays[f"in_{name}"] = a
        args.append(nc.dram_tensor(f"in_{name}", a.shape, mybir.dt.from_np(a.dtype), kind="ExternalInput").ap())
    out = nc.dram_tensor("out_x", (NB, T_SEQ, C), F32, kind="ExternalOutput").ap()
    macaron(nc, *args, out)
    r = run_bass_kernel_spmd(nc, [arrays], core_ids=[0])
    return r.results[0]["out_x"]
```

```python
from contextlib import ExitStack

import concourse.bass as bass
from concourse import mybir

F32 = mybir.dt.float32
F16 = mybir.dt.float16
I32 = mybir.dt.int32
ALU = mybir.AluOpType
ACT = mybir.ActivationFunctionType
AX = mybir.AxisListType
ds = bass.ds

P = 128
NB, T_SEQ, C = 4, 512, 128
N = NB * T_SEQ
NT = N // P
TG = T_SEQ // P
E = 8
HID = 512
J = HID // P
U = 8
G = (2 * N + E * (P - 1)) // P
K = 2
KN = K * N
NC = K * NT
BODIES = -(-G // U)
LAST = (BODIES - 1) * U
RUNS = [len(range(k, G, U)) for k in range(U)]
AHEAD = 24
EPS = 1e-5
X_SCALE = 1024.0
TOP = 2.0 ** 14
TINY = 2.0 ** -40
BIG = 1e30
LAYERS = 2
HELD_AT = ((0, 2), (1, 1))
GATE_BANKS = (6, 7, 0, 1)
BIAS_BANKS = (2, 3, 6, 7)
ACT_GATES = (((1,), (0, 1), (0, 1), (0, 1)), ((1,), (1,), (1,), (1,)))
assert C == P and G - LAST >= 4


def macaron(nc, x_in, gamma, beta, wg, bg, wc, bc, wfc_s, bfc_s, wproj_s, bproj_s, wr, wfc, bfc, wproj, bproj, out):
    x_rows = x_in.rearrange("b (t p) c -> p (b t) c", p=P)
    out_rows = out.rearrange("b (t p) c -> p (b t) c", p=P)
    xsplit_dram = [nc.dram_tensor(f"xsplit_{i}", (N, 2 * C), F16, kind="Internal").ap() for i in range(LAYERS)]
    routed_dram = [nc.dram_tensor(f"routed_{i}", (KN + G * P, C), F32, kind="Internal").ap() for i in range(LAYERS)]

    with ExitStack() as ctx:
        def sb(name, shape, dt=F32):
            return ctx.enter_context(nc.sbuf_tensor(name, shape, dt))

        def sem(name):
            return ctx.enter_context(nc.semaphore(name))

        ps = ctx.enter_context(nc.psum_tensor("ps", [P, 8 * 512], F32))

        def bank(b, n=512):
            return ps[:, b * 512:b * 512 + n]

        xs = sb("xs", [P, N])
        xn = sb("xn", [P, N])
        xsplit = sb("xsplit", [P, NT, 2, C], F16)
        xT = sb("xT", [P, 2, N], F16)
        xT32 = xT[:, :, :].bitcast(F32)

        wraw = sb("wraw", [P, 2 * (E + 1) * HID])
        w1raw = wraw[:, 0:(E + 1) * HID].rearrange("p (e h) -> p e h", e=E + 1)
        w2raw = wraw[:, (E + 1) * HID:].rearrange("p (e j c) -> p e j c", e=E + 1, j=J)
        w1 = sb("w1", [P, E + 1, 2, HID], F16)
        w2 = sb("w2", [P, E + 1, J, 2, C], F16)
        w1f = w1[:, :, :, :].rearrange("p e s h -> p (e s h)")
        w2f = w2[:, :, :, :, :].rearrange("p e j s c -> p (e j s c)")
        wr_raw = sb("wr_raw", [P, E])
        wr16 = sb("wr16", [P, 2, E], F16)
        b1rows = sb("b1rows", [(E + 1) * J, P])
        b1_all = sb("b1_all", [P, E * HID])
        b1T = sb("b1T", [P, (E + 1) * J])
        b2rows = sb("b2rows", [E + 1, C])
        w_att_raw = sb("w_att_raw", [P, 2, C])
        w_att = sb("w_att", [P, 2, C])
        cols = sb("cols", [P, 4])
        half_bg = sb("half_bg", [P, 1])

        ident = sb("ident", [P, P])
        ident16 = sb("ident16", [P, P], F16)
        before = sb("before", [P, P], F16)
        ones16 = sb("ones16", [P, P], F16)
        ones_row = sb("ones_row", [4, P])
        rank8 = sb("rank8", [P, E])
        lane = sb("lane", [P, P], F16)
        slot_tile = sb("slot_tile", [P, G], F16)
        pair_no = sb("pair_no", [P, NC], F16)
        own_lane = sb("own_lane", [P, 1])
        carry = sb("carry", [P, E * NT])
        spare_row = sb("spare_row", [P, G])
        minus_half = sb("minus_half", [P, K, TG])

        bn = sb("bn", [P, NT, 6])
        moments = sb("moments", [P, NT, 2])
        veps = sb("veps", [P, NT])
        rstd = sb("rstd", [P, NT])
        att_v = sb("att_v", [P, 2, NT])
        att_q = sb("att_q", [P, 2, NT])
        att_r = sb("att_r", [P, 2, NT])

        peak = sb("peak", [P, 6])
        peak_max = sb("peak_max", [4, 1])
        peak_diag = sb("peak_diag", [4, 4])
        peak_all = sb("peak_all", [P, 6])
        bound = sb("bound", [P, 8])
        pow2 = sb("pow2", [P, 8])
        inv = sb("inv", [P, 8])
        scale_w = sb("scale_w", [P, 8])
        un = sb("un", [P, 8])

        logits = sb("logits", [P, NT, E])
        logits2 = sb("logits2", [P, NT, E])
        pick = sb("pick", [P, 3, NT * E])
        best = sb("best", [P, K, NT])
        top_rank = sb("top_rank", [P, NT])
        chosen = sb("chosen", [P, K, NT, E])
        gap = sb("gap", [P, NT])
        gap_tanh = sb("gap_tanh", [P, NT])
        gate = sb("gate", [P, K, NT])
        gate_un = sb("gate_un", [P, K, NT])
        gates = sb("gates", [P, NT, E + 1])
        gates_k = sb("gates_k", [P, K, NT, E])
        gatesT = sb("gatesT", [E + 1, N])
        used = sb("used", [P, E * NT], F16)
        upto = sb("upto", [P, E * NT])
        ahead = sb("ahead", [P, E * NT], F16)
        total = sb("total", [P, E], F16)
        tiles_i = sb("tiles_i", [P, 2, E], I32)
        tiles = sb("tiles", [P, E])
        tile_end = sb("tile_end", [P, E])
        tile_start = sb("tile_start", [P, E])
        ones8 = sb("ones8", [P, E])
        slot_of = sb("slot_of", [P, E * NT])
        slot_k = sb("slot_k", [P, K, NT * E])
        slot = sb("slot", [P, NC])
        slot_i = sb("slot_i", [P, 3, NC], I32)
        slot_g = sb("slot_g", [P, NC], F16)
        slot_p = sb("slot_p", [P, NC], F16)
        in_tile = sb("in_tile", [P, NC, G], F16)
        in_tile_id = sb("in_tile_id", [P, NC, 2, G], F16)
        held = sb("held", [P, 2, G])
        row_id = sb("row_id", [P, G])
        rt = sb("rt", [P, 5, G])
        ended = sb("ended", [P, G, E])
        gather_row = sb("gather_row", [P, G], I32)
        scatter_row = sb("scatter_row", [P, G], I32)
        tile_expert = sb("tile_expert", [P, G], I32)

        h_sh = sb("h_sh", [P, J, T_SEQ])
        hs_sh = sb("hs_sh", [P, 2, J, T_SEQ], F16)
        xg = sb("xg", [P, G * 2 * C], F16)
        in_lane = xg[:, 0:NC * P].rearrange("p (n l) -> p n l", n=NC)
        xatt = xg[:, 0:2 * N].bitcast(F32)
        routed = wraw[:, 0:K * N]
        xgT = sb("xgT", [P, 2, 2 * P], F16)
        xgT32 = xgT[:, :, :].bitcast(F32)
        h = h_sh[:, 0:2]
        hs = hs_sh[:, :, :, :].rearrange("p s j t -> p j s t")[:, 0:2]
        up_sum = h_sh[:, 2:4]
        y_low = sb("y_low", [P, 2, C])
        y = sb("y", [P, U, C])

        att = wraw[:, K * N:K * N + 5 * 2 * T_SEQ].rearrange("p (k b t) -> p k b t", k=5, b=2)
        normT, zt, at_, bt, ht = (att[:, k] for k in range(5))
        zh = h_sh[:, 0:2]

        x_loaded = [sem(f"x_loaded_{g}") for g in range(NB)]
        small_loaded = sem("small_loaded")
        shared_loaded = sem("shared_loaded")
        routed_loaded = sem("routed_loaded")
        consts_made = sem("consts_made")
        pool_step = sem("pool_step")
        dve_step = sem("dve_step")
        var_ready = sem("var_ready")
        rstd_ready = sem("rstd_ready")
        ln_ready = sem("ln_ready")
        ln_high = sem("ln_high")
        att_var_ready = sem("att_var_ready")
        att_rstd_ready = sem("att_rstd_ready")
        xatt_ready = sem("xatt_ready")
        peaks_ready = sem("peaks_ready")
        peaksT_ready = sem("peaksT_ready")
        peak_diag_ready = sem("peak_diag_ready")
        peaks_spread = sem("peaks_spread")
        att_w_turned = sem("att_w_turned")
        scales_ready = sem("scales_ready")
        weights_hi = sem("weights_hi")
        router_w_ready = sem("router_w_ready")
        weights_split = sem("weights_split")
        weights_low = sem("weights_low")
        xsplit_ready = sem("xsplit_ready")
        xsplit_stored = sem("xsplit_stored")
        xT_turned = sem("xT_turned")
        xT_ready = sem("xT_ready")
        logits_ready = sem("logits_ready")
        used_ready = sem("used_ready")
        rank_ready = sem("rank_ready")
        gap_ready = sem("gap_ready")
        gap_tanh_ready = sem("gap_tanh_ready")
        in_tile_ready = sem("in_tile_ready")
        pair_ids_ready = sem("pair_ids_ready")
        lane_ids_ready = sem("lane_ids_ready")
        in_lane_ready = sem("in_lane_ready")
        held_ready = sem("held_ready")
        rows_ready = sem("rows_ready")
        experts_ready = sem("experts_ready")
        gates_ready = sem("gates_ready")
        gates_turned = sem("gates_turned")
        gatesT_ready = sem("gatesT_ready")
        bias_ready = sem("bias_ready")
        sh_up = sem("sh_up")
        sh_gelu = sem("sh_gelu")
        sh_high = sem("sh_high")
        sh_split = sem("sh_split")
        sh_down = sem("sh_down")
        gathered = [sem(f"gathered_{k}") for k in range(U)]
        scattered = [sem(f"scattered_{k}") for k in range(U)]
        xg_turned = sem("xg_turned")
        xgT_ready = sem("xgT_ready")
        b1_loaded = sem("b1_loaded")
        sum_ready = sem("sum_ready")
        h_slots_turned = sem("h_slots_turned")
        high_ready = sem("high_ready")
        y_low_ready = sem("y_low_ready")
        up_ready = sem("up_ready")
        gelu_ready = sem("gelu_ready")
        split_ready = sem("split_ready")
        down_ready = sem("down_ready")
        y_ready = sem("y_ready")
        routed_back = [sem(f"routed_back_{g}") for g in range(NB)]
        gate_un_ready = sem("gate_un_ready")
        products_ready = sem("products_ready")
        x_done = sem("x_done")
        norm_ready = sem("norm_ready")
        norm_turned = sem("norm_turned")
        normT_ready = sem("normT_ready")
        gates_in = sem("gates_in")
        cand_in = sem("cand_in")
        tanh_ready = sem("tanh_ready")
        z_ready = sem("z_ready")
        hT_ready = sem("hT_ready")
        h_turned = sem("h_turned")
        x_sum_ready = sem("x_sum_ready")
        out_stored = sem("out_stored")

        SMALL = 10
        block = ctx.enter_context(nc.Block())

        class Steps:

            def __init__(self, eng, own_sem):
                self.eng, self.own_sem, self.count = eng, own_sem, 0

            def link(self, ins):
                ins.then_inc(self.own_sem, 1)
                self.count += 1
                self.eng.wait_ge(self.own_sem, self.count)

        @block.sync
        def _(sp):
            for g in range(NB):
                sp.dma_start(xs[:, g * T_SEQ:(g + 1) * T_SEQ].rearrange("p (t c) -> p t c", c=C),
                             x_rows[:, g * TG:(g + 1) * TG]).then_inc(x_loaded[g], 16)
            sp.dma_start(w1raw[:, E, :], wfc_s).then_inc(shared_loaded, 16)
            sp.dma_start(w2raw[:, E], wproj_s.rearrange("(j p) c -> p j c", p=P)).then_inc(shared_loaded, 16)
            for g in range(NB):
                sp.wait_ge(x_loaded[g], 16)
            sp.wait_ge(shared_loaded, 32)
            sp.dma_start(w1raw[:, 0:E], wfc.rearrange("e c h -> c e h")).then_inc(routed_loaded, 16)
            sp.dma_start(w2raw[:, 0:E], wproj.rearrange("e (j p) c -> p e j c", p=P)).then_inc(routed_loaded, 16)
            sp.dma_start(b1_all[:, :], bfc.rearrange("(a e) h -> a (e h)", a=1).broadcast_to([P, E * HID])
                         ).then_inc(b1_loaded, 16)
            for layer in range(LAYERS):
                with sp.Fori(0, NB) as g:
                    sp.wait_ge(xsplit_ready, layer * NB + g + 1)
                    sp.dma_start(xsplit_dram[layer][ds(g * T_SEQ, T_SEQ), :].rearrange("(t p) c -> p t c", p=P),
                                 xsplit[:, ds(g * TG, TG)].rearrange("p t s c -> p t (s c)")).then_inc(xsplit_stored, 16)
                for k in range(U):
                    sp.wait_ge(scattered[k], 16 * RUNS[k] * (layer + 1))
                for g in range(NB):
                    for k in range(K):
                        sp.dma_start(routed[:, k * N + g * T_SEQ:k * N + (g + 1) * T_SEQ].rearrange(
                                         "p (t c) -> p t c", c=C),
                                     routed_dram[layer][k * N + g * T_SEQ:k * N + (g + 1) * T_SEQ, :].rearrange(
                                         "(t p) c -> p t c", p=P)).then_inc(routed_back[g], 16)
            with sp.Fori(0, NB) as g:
                sp.wait_ge(x_done, g + 1)
                sp.dma_start(out_rows[:, ds(g * TG, TG), :],
                             xs[:, ds(g * T_SEQ, T_SEQ)].rearrange("p (t c) -> p t c", c=C)).then_inc(out_stored, 16)
            sp.wait_ge(out_stored, 16 * NB)
            sp.wait_ge(xsplit_stored, 16 * NB * LAYERS)

        @block.gpsimd
        def _(pool):
            steps = Steps(pool, pool_step)
            pool.memset(ident[:, :], 0.0)
            pool.memset(before[:, :], 1.0)
            pool.memset(ones16[:, :], 1.0)
            pool.memset(ones_row[:, :], 1.0)
            pool.memset(ones8[:, :], 1.0)
            pool.memset(carry[:, :], 1.0)
            pool.memset(minus_half[:, :, :], -0.5)
            pool.memset(peak[:, :], 0.0)
            pool.memset(gates[:, :, E:E + 1], 0.5)
            pool.iota(rank8[:, :], [[-1, E]], base=E, channel_multiplier=0, allow_small_or_imprecise_dtypes=True)
            pool.iota(lane[:, :], [[1, P]], base=0, channel_multiplier=0, allow_small_or_imprecise_dtypes=True)
            pool.iota(slot_tile[:, :], [[1, G]], base=0, channel_multiplier=0, allow_small_or_imprecise_dtypes=True)
            pool.iota(pair_no[:, :], [[1, NC]], base=1, channel_multiplier=0, allow_small_or_imprecise_dtypes=True)
            pool.iota(own_lane[:, :], [[0, 1]], base=0, channel_multiplier=1, allow_small_or_imprecise_dtypes=True)
            steps.link(pool.iota(spare_row[:, :], [[P, G]], base=KN + P, channel_multiplier=1,
                                 allow_small_or_imprecise_dtypes=True))
            pool.memset(carry[:, :].rearrange("p (e t) -> p e t", e=E)[:, :, 0:1], 0.0)
            pool.affine_select(out=before[:, :], in_=before[:, :], compare_op=ALU.is_gt, fill=0.0, base=0,
                               pattern=[[1, P]], channel_multiplier=-1)
            steps.link(pool.affine_select(out=ident[:, :], in_=ident[:, :], compare_op=ALU.not_equal, fill=1.0,
                                          base=0, pattern=[[-1, P]], channel_multiplier=1))
            pool.tensor_copy(ident16[:, :], ident[:, :]).then_inc(consts_made, 1)

            def ln_rstd(layer, g):
                at = slice(g * TG, (g + 1) * TG)
                pool.wait_ge(var_ready, layer * NB + g + 1)
                steps.link(pool.tensor_scalar(veps[:, at], moments[:, at, 1], EPS, X_SCALE ** -2.0, ALU.add, ALU.mult))
                pool.tensor_tensor(rstd[:, at], veps[:, at], minus_half[:, 0], ALU.pow).then_inc(rstd_ready, 1)

            def att_rstd(g):
                at = slice(g * TG, (g + 1) * TG)
                pool.wait_ge(att_var_ready, g + 1)
                pool.tensor_tensor(att_r[:, :, at], att_q[:, :, at], minus_half[:, :, :], ALU.pow
                                   ).then_inc(att_rstd_ready, 1)

            for g in range(NB):
                ln_rstd(0, g)

            for layer in range(LAYERS):
                pool.wait_ge(in_tile_ready, layer + 1)
                pool.tensor_tensor(in_tile_id[:, :, 0, :], in_tile[:, :, :],
                                   pair_no[:, :].unsqueeze(2).broadcast_to([P, NC, G]), ALU.mult
                                   ).then_inc(pair_ids_ready, 1)

                pool.wait_ge(rows_ready, layer + 1)
                pool.wait_ge(xsplit_stored, 16 * NB * (layer + 1))

                def gather(i):
                    k, n = i % U, i // U
                    if layer or n:
                        pool.wait_ge(gathered[k], 16 * (layer * RUNS[k] + n))
                    pool.indirect_dma_start(
                        out=xg[:, i * 2 * C:(i + 1) * 2 * C], out_offset=None, in_=xsplit_dram[layer][:, :],
                        in_offset=bass.IndirectOffsetOnAxis(ap=gather_row[:, i:i + 1], axis=0),
                    ).then_inc(gathered[k], 16)

                for i in range(AHEAD):
                    gather(i)
                for i in range(G):
                    pool.wait_ge(y_ready, layer * G + i + 1)
                    pool.indirect_dma_start(
                        out=routed_dram[layer][:, :],
                        out_offset=bass.IndirectOffsetOnAxis(ap=scatter_row[:, i:i + 1], axis=0),
                        in_=y[:, i % U, :], in_offset=None,
                    ).then_inc(scattered[i % U], 16)
                    if i + AHEAD < G:
                        gather(i + AHEAD)
                if layer == 0:
                    def add_att(b):
                        at = slice(b * T_SEQ, (b + 1) * T_SEQ)
                        pool.wait_ge(xatt_ready, b + 1)
                        pool.tensor_tensor(xs[:, at], xs[:, at], xatt[:, at], ALU.add).then_inc(x_sum_ready, 1)

                    att_rstd(0)
                    for b in range(1, NB):
                        att_rstd(b)
                        add_att(b - 1)
                    add_att(NB - 1)
                    for b in range(NB):
                        ln_rstd(1, b)

        @block.scalar
        def _(act):
            small = [(wr_raw[:, :], wr), (b1rows[0:E * J, :], bfc.rearrange("e (j p) -> (e j) p", p=P)),
                     (b1rows[E * J:, :], bfc_s.rearrange("(j p) -> j p", p=P)), (b2rows[0:E, :], bproj),
                     (b2rows[E:E + 1, :], bproj_s.rearrange("(a c) -> a c", a=1)),
                     (w_att_raw[:, 0], wg), (w_att_raw[:, 1], wc)]
            small += [(cols[:, n:n + 1], v.rearrange("(p a) -> p a", a=1)) for n, v in enumerate((gamma, beta, bg))]
            assert len(small) == SMALL
            for dst, src in small:
                act.dma_start(dst, src).then_inc(small_loaded, 16)
            act.dma_start(cols[:, 3:4], bc.rearrange("(p a) -> p a", a=1)).then_inc(small_loaded, 16)
            act.preload_act_table(ACT.Gelu_apprx_tanh)

            def ln_hi(layer, g):
                act.wait_ge(ln_ready, layer * NB + g + 1)
                act.copy(xsplit[:, g * TG:(g + 1) * TG, 0, :],
                         xn[:, g * T_SEQ:(g + 1) * T_SEQ].rearrange("p (t c) -> p t c", c=C)).then_inc(ln_high, 1)

            def move_xT(layer, g):
                act.wait_ge(xT_turned, layer * NB + g + 1)
                act.copy(xT32[:, :, g * (T_SEQ // 2):(g + 1) * (T_SEQ // 2)],
                         bank(4 + g % 2).rearrange("p (s t) -> p s t", s=2)).then_inc(xT_ready, 1)

            def sh_act(layer, g, j):
                act.wait_ge(sh_up, layer * NB * J + g * J + j + 1)
                act.activation(h_sh[:, j, :], bank(j), ACT.Gelu_apprx_tanh, scale=un[:, 0:1],
                               bias=b1T[:, E * J + j:E * J + j + 1]).then_inc(sh_gelu, 1)

            def sh_hi(layer, g, j):
                act.wait_ge(sh_gelu, layer * NB * J + g * J + j + 1)
                act.activation(hs_sh[:, 0, j, :], h_sh[:, j, :], ACT.Identity,
                               scale=scale_w[:, 2:3]).then_inc(sh_high, 1)

            for g in range(NB):
                ln_hi(0, g)
                if g:
                    move_xT(0, g - 1)
            move_xT(0, NB - 1)

            for layer in range(LAYERS):
                def high_weights(which, q):
                    e = slice(q * E // NB, (q + 1) * E // NB)
                    act.wait_ge(scales_ready, 1)
                    if which == 0:
                        act.activation(w1[:, e, 0, :], w1raw[:, e], ACT.Identity,
                                       scale=scale_w[:, 4:5]).then_inc(weights_hi, 1)
                    else:
                        act.activation(w2[:, e, :, 0, :], w2raw[:, e], ACT.Identity,
                                       scale=scale_w[:, 5:6]).then_inc(weights_hi, 1)

                for j in range(2 * layer, 3):
                    sh_act(layer, 0, j)
                    if j and not layer:
                        sh_hi(layer, 0, j - 1)
                act.wait_ge(gap_ready, layer + 1)
                act.activation(gap_tanh[:, :], gap[:, :], ACT.Tanh, scale=un[:, 5:6]).then_inc(gap_tanh_ready, 1)
                sh_act(layer, 0, 3)
                sh_hi(layer, 0, 2)
                sh_hi(layer, 0, 3)

                for g in range(1, NB):
                    sh_act(layer, g, 0)
                    for j in range(J):
                        if j + 1 < J:
                            sh_act(layer, g, j + 1)
                        sh_hi(layer, g, j)
                    if layer == 0 and g <= 2:
                        for q in range(NB):
                            high_weights(g - 1, q)

                def gelu(i, par):
                    act.wait_ge(sum_ready, layer * G + i + 1)
                    for half in range(2):
                        at = slice(half * HID // 2, (half + 1) * HID // 2)
                        act.activation(h[:, par, at], up_sum[:, par, at], ACT.Gelu_apprx_tanh).then_inc(gelu_ready, 1)

                def move_xg(i, par):
                    act.wait_ge(xg_turned, layer * G + i + 1)
                    act.copy(xgT32[:, par, :], bank(6 + par, P)).then_inc(xgT_ready, 1)

                def high(i, par):
                    act.wait_ge(h_slots_turned, layer * G + i + 1)
                    act.activation(hs[:, par, 0, :], bank(2 + par), ACT.Identity,
                                   scale=scale_w[:, 6:7]).then_inc(high_ready, 1)

                def move_low(i, par):
                    act.wait_ge(down_ready, layer * G + i + 1)
                    act.copy(y_low[:, par, :], bank(4 + par)[:, C:2 * C]).then_inc(y_low_ready, 1)

                move_xg(0, 0)
                move_xg(1, 1)
                gelu(0, 0)
                move_xg(2, 0)
                gelu(1, 1)
                high(0, 0)
                move_xg(3, 1)
                with act.Fori(0, BODIES - 1) as n:
                    for k in range(U):
                        high(n * U + k + 1, (k + 1) % 2)
                        gelu(n * U + k + 2, k % 2)
                        move_low(n * U + k, k % 2)
                        move_xg(n * U + k + 4, k % 2)
                for i in range(LAST, G):
                    if i + 1 < G:
                        high(i + 1, (i + 1) % 2)
                    if i + 2 < G:
                        gelu(i + 2, i % 2)
                    move_low(i, i % 2)
                    if i + 4 < G:
                        move_xg(i + 4, i % 2)

                for g in range(NB):
                    act.wait_ge(gates_turned, layer * NB + g + 1)
                    act.copy(gatesT[:, g * T_SEQ:(g + 1) * T_SEQ], bank(GATE_BANKS[g])[0:E + 1, :]
                             ).then_inc(gatesT_ready, 1)
                act.wait_ge(gate_un_ready, layer + 1)
                for g in range(NB):
                    act.wait_ge(routed_back[g], 16 * K * (layer + 1))
                    for k in ACT_GATES[layer][g]:
                        for t in range(g * TG, (g + 1) * TG):
                            at = slice(k * N + t * C, k * N + (t + 1) * C)
                            ins = act.activation(routed[:, at], routed[:, at], ACT.Identity,
                                                 scale=gate_un[:, k, t:t + 1])
                    ins.then_inc(products_ready, 1)

                if layer == 0:
                    def second_norm(b):
                        act.wait_ge(xatt_ready, b + 1)
                        for t in range(b * TG, (b + 1) * TG):
                            ins = act.activation(xn[:, t * C:(t + 1) * C], xatt[:, t * C:(t + 1) * C],
                                                 ACT.Identity, scale=att_r[:, 1, t:t + 1])
                        ins.then_inc(norm_ready, 1)

                    def move_norm(b):
                        act.wait_ge(norm_turned, b + 1)
                        act.activation(normT[:, b % 2], bank(0), ACT.Identity, scale=cols[:, 0:1],
                                       bias=cols[:, 1:2]).then_inc(normT_ready, 1)

                    def gate_tanh(b):
                        act.wait_ge(gates_in, b + 1)
                        act.activation(zh[:, b % 2], bank(1), ACT.Tanh, scale=0.5,
                                       bias=half_bg[:, 0:1]).then_inc(tanh_ready, 1)

                    def gates_z(b):
                        act.wait_ge(tanh_ready, b + 1)
                        if b >= 2:
                            act.wait_ge(hT_ready, b - 1)
                        act.activation(zt[:, b % 2], zh[:, b % 2], ACT.Copy, scale=0.5, bias=0.5)
                        act.activation(at_[:, b % 2], zh[:, b % 2], ACT.Copy, scale=-0.5,
                                       bias=0.5).then_inc(z_ready, 1)

                    second_norm(0)
                    move_norm(0)
                    second_norm(1)
                    gate_tanh(0)
                    gates_z(0)
                    move_norm(1)
                    second_norm(2)
                    gate_tanh(1)
                    gates_z(1)
                    move_norm(2)
                    second_norm(3)
                    gate_tanh(2)
                    gates_z(2)
                    move_norm(3)
                    ln_hi(1, 0)
                    gate_tanh(3)
                    gates_z(3)
                    move_xT(1, 0)
                    ln_hi(1, 1)
                    move_xT(1, 1)
                    ln_hi(1, 2)
                    act.wait_ge(z_ready, NB)
                    sh_act(1, 0, 0)
                    sh_act(1, 0, 1)
                    sh_hi(1, 0, 0)
                    move_xT(1, 2)
                    ln_hi(1, 3)
                    sh_hi(1, 0, 1)
                    move_xT(1, 3)

        @block.vector
        def _(dve):
            steps = Steps(dve, dve_step)
            regs = [dve.alloc_register(f"dve_expert_{k}") for k in range(U)]
            link = steps.link
            def add_stats(g):
                for t in range(g * TG, (g + 1) * TG):
                    ins = dve.bn_stats(bn[:, t, :], xs[:, t * C:(t + 1) * C])
                link(ins)
                for t in range(g * TG, (g + 1) * TG):
                    ins = dve.bn_aggr(moments[:, t, :], bn[:, t, :])
                return ins

            def normalize(dst, factor, g):
                for t in range(g * TG, (g + 1) * TG):
                    ins = dve.tensor_scalar(dst[:, t * C:(t + 1) * C], xs[:, t * C:(t + 1) * C], moments[:, t, 0:1],
                                            factor[:, t:t + 1], ALU.subtract, ALU.mult)
                return ins

            def ln_norm(layer, g):
                dve.wait_ge(rstd_ready, layer * NB + g + 1)
                normalize(xn, rstd, g).then_inc(ln_ready, 1)

            def ln_low(layer, g):
                dve.wait_ge(ln_high, layer * NB + g + 1)
                dve.tensor_tensor(xsplit[:, g * TG:(g + 1) * TG, 1, :],
                                  xn[:, g * T_SEQ:(g + 1) * T_SEQ].rearrange("p (t c) -> p t c", c=C),
                                  xsplit[:, g * TG:(g + 1) * TG, 0, :], ALU.subtract).then_inc(xsplit_ready, 1)

            def spread_peaks(n, first, rnd):
                dve.wait_ge(peaksT_ready, rnd)
                link(dve.tensor_reduce(peak_max[0:n, :], bank(7)[0:n, 0:P], AX.X, ALU.max))
                dve.tensor_scalar(peak_diag[0:n, 0:n], ident[0:n, 0:n], peak_max[0:n, 0:1], None,
                                  ALU.mult).then_inc(peak_diag_ready, 1)
                dve.wait_ge(peaks_spread, rnd)
                dve.tensor_copy(peak_all[:, first:first + n], bank(7, n))
                link(dve.tensor_copy(bound[:, first:first + n], bank(7, n)))

            def scales(c, n, u):
                at = slice(c, c + n)
                link(dve.scalar_tensor_tensor(bound[:, c + 2:c + 3], bound[:, c:c + 1], float(P), peak_all[:, 2:3],
                                              ALU.mult, ALU.add))
                link(dve.tensor_scalar(pow2[:, at].bitcast(I32), bound[:, at].bitcast(I32), 0x7F800000, None,
                                       ALU.bitwise_and))
                link(dve.tensor_scalar(pow2[:, at], pow2[:, at], TINY, None, ALU.max))
                dve.tensor_scalar(un[:, u:u + 1], pow2[:, c:c + 1], 1.0 / (TOP * X_SCALE), None, ALU.mult)
                dve.scalar_tensor_tensor(un[:, u + 1:u + 2], pow2[:, c + 2:c + 3], TOP ** -2.0, pow2[:, c + 1:c + 2],
                                         ALU.mult, ALU.mult)
                link(dve.reciprocal(inv[:, at], pow2[:, at]))
                link(dve.tensor_scalar(scale_w[:, at], inv[:, at], TOP, None, ALU.mult))

            def first_scales():
                dve.wait_ge(shared_loaded, 32)
                dve.wait_ge(small_loaded, 16 * (SMALL + 1))
                dve.tensor_reduce(peak[:, 0:1], w1raw[:, E], AX.X, ALU.max, apply_absolute_value=True)
                dve.tensor_reduce(peak[:, 1:2], w2raw[:, E].rearrange("p j c -> p (j c)"), AX.X, ALU.max,
                                  apply_absolute_value=True)
                dve.tensor_reduce(peak[:, 3:4], wr_raw[:, :], AX.X, ALU.max, apply_absolute_value=True)
                dve.tensor_reduce(peak[0:(E + 1) * J, 2:3], b1rows[:, :], AX.X, ALU.max,
                                  apply_absolute_value=True).then_inc(peaks_ready, 1)
                spread_peaks(4, 0, 1)
                scales(0, 4, 0)
                dve.tensor_scalar(un[:, 4:5], un[:, 1:2], 0.5, None, ALU.mult)
                dve.tensor_scalar(un[:, 5:6], pow2[:, 3:4], 0.5 / (TOP * X_SCALE), None, ALU.mult)
                link(dve.tensor_scalar(wr16[:, 0, :], wr_raw[:, :], scale_w[:, 3:4], None, ALU.mult))
                dve.scalar_tensor_tensor(wr16[:, 1, :], wr_raw[:, :], scale_w[:, 3:4], wr16[:, 0, :], ALU.mult,
                                         ALU.subtract).then_inc(router_w_ready, 1)
                dve.tensor_scalar(half_bg[:, :], cols[:, 2:3], 0.5, None, ALU.mult)
                dve.wait_ge(att_w_turned, 1)
                dve.tensor_copy(b1T[:, :], bank(0, (E + 1) * J))
                link(dve.tensor_copy(w_att[:, :, :].rearrange("p k c -> p (k c)"), bank(1, 2 * C)))

            def split_shared():
                for raw, hi, lo, col in ((w1raw[:, E], w1[:, E, 0], w1[:, E, 1], 0),
                                         (w2raw[:, E], w2[:, E, :, 0], w2[:, E, :, 1], 1)):
                    link(dve.tensor_scalar(hi, raw, scale_w[:, col:col + 1], None, ALU.mult))
                    ins = dve.scalar_tensor_tensor(lo, raw, scale_w[:, col:col + 1], hi, ALU.mult, ALU.subtract)
                ins.then_inc(weights_split, 1)

            def routed_scales():
                spread_peaks(2, 4, 2)
                scales(4, 3, 2)
                dve.memset(pick[:, 2, 0:1], 0.0).then_inc(scales_ready, 1)

            def choose(k, src):
                v = [pick[:, n, :].rearrange("p (t e) -> p t e", e=E) for n in range(2)]
                ranks = rank8[:, :].unsqueeze(1).broadcast_to([P, NT, E])
                link(dve.tensor_reduce(best[:, k, :], src, AX.X, ALU.max))
                link(dve.tensor_tensor(v[0], src, best[:, k, :].unsqueeze(2).broadcast_to([P, NT, E]), ALU.is_equal))
                link(dve.tensor_tensor(v[1], v[0], ranks, ALU.mult))
                link(dve.tensor_reduce(top_rank[:, :], v[1], AX.X, ALU.max))
                link(dve.tensor_tensor(chosen[:, k], ranks, top_rank[:, :].unsqueeze(2).broadcast_to([P, NT, E]),
                                       ALU.is_equal))

            def sh_lo(layer, g, j):
                dve.wait_ge(sh_high, layer * NB * J + g * J + j + 1)
                dve.scalar_tensor_tensor(hs_sh[:, 1, j, :], h_sh[:, j, :], scale_w[:, 2:3], hs_sh[:, 0, j, :],
                                         ALU.mult, ALU.subtract).then_inc(sh_split, 1)

            def sh_add(layer, g):
                at = slice(g * T_SEQ, (g + 1) * T_SEQ)
                dve.wait_ge(sh_down, layer * NB + g + 1)
                dve.scalar_tensor_tensor(xs[:, at], bank(4 + g % 2), un[:, 4:5], xs[:, at], ALU.mult, ALU.add)

            def low_weights(which, q):
                e = slice(q * E // NB, (q + 1) * E // NB)
                dve.wait_ge(weights_hi, which * NB + q + 1)
                if which == 0:
                    return dve.scalar_tensor_tensor(w1[:, e, 1, :], w1raw[:, e], scale_w[:, 4:5], w1[:, e, 0, :],
                                                    ALU.mult, ALU.subtract)
                return dve.scalar_tensor_tensor(w2[:, e, :, 1, :], w2raw[:, e], scale_w[:, 5:6], w2[:, e, :, 0, :],
                                                ALU.mult, ALU.subtract)

            def shared_rest(layer):
                for g in range(1, NB):
                    for j in range(J):
                        if not (layer and g == 1 and j < 3):
                            sh_lo(layer, g, j)
                        if j == 1 and layer:
                            sh_add(layer, g - 1)
                    if layer == 0 and g <= 2:
                        for q in range(NB):
                            ins = low_weights(g - 1, q)
                    if layer == 0:
                        sh_add(layer, g - 1)
                if layer == 0:
                    ins.then_inc(weights_low, 1)

            def route(layer):
                dve.wait_ge(logits_ready, NB * (layer + 1))
                link(dve.tensor_reduce(logits[:, :, :],
                                       bank(7, NT * 2 * E).rearrange("p (t s e) -> p t e s", s=2, e=E),
                                       AX.X, ALU.add))
                choose(0, logits[:, :, :])
                link(dve.scalar_tensor_tensor(logits2[:, :, :], chosen[:, 0], -BIG, logits[:, :, :], ALU.mult,
                                              ALU.add))
                choose(1, logits2[:, :, :])
                dve.tensor_tensor(gap[:, :], best[:, 1, :], best[:, 0, :], ALU.subtract).then_inc(gap_ready, 1)
                link(dve.tensor_tensor(used[:, :].rearrange("p (e t) -> p t e", e=E), chosen[:, 0], chosen[:, 1],
                                       ALU.add))
                link(dve.tensor_tensor_scan(upto[:, :], carry[:, :], used[:, :], 0.0, ALU.mult, ALU.add))
                dve.tensor_copy(total[:, :].unsqueeze(2), upto[:, :].rearrange("p (e t) -> p e t", e=E)[:, :, NT - 1:NT])
                dve.tensor_tensor(ahead[:, :], upto[:, :], used[:, :], ALU.subtract).then_inc(used_ready, 1)
                make_gates(layer)
                sh_lo(layer, 0, 2 * layer)
                dve.wait_ge(rank_ready, layer + 1)
                link(dve.tensor_scalar(tiles_i[:, 0, :], bank(6)[:, P:P + E], float(P - 1), None, ALU.add))
                link(dve.tensor_scalar(tiles_i[:, 1, :], tiles_i[:, 0, :], 7, None, ALU.logical_shift_right))
                link(dve.tensor_copy(tiles[:, :], tiles_i[:, 1, :]))
                link(dve.tensor_tensor_scan(tile_end[:, :], ones8[:, :], tiles[:, :], 0.0, ALU.mult, ALU.add))
                link(dve.tensor_tensor(tile_start[:, :], tile_end[:, :], tiles[:, :], ALU.subtract))
                link(dve.scalar_tensor_tensor(slot_of[:, :].rearrange("p (e t) -> p e t", e=E),
                                              tile_start[:, :].unsqueeze(2).broadcast_to([P, E, NT]), float(P),
                                              bank(6, P).rearrange("p (e t) -> p e t", e=E), ALU.mult, ALU.add))
                sk = [slot_k[:, k, :].rearrange("p (t e) -> p t e", e=E) for k in range(K)]
                for k in range(K):
                    ins = dve.tensor_tensor(sk[k], chosen[:, k], slot_of[:, :].rearrange("p (e t) -> p t e", e=E),
                                            ALU.mult)
                link(ins)
                for k in range(K):
                    ins = dve.tensor_reduce(slot[:, k * NT:(k + 1) * NT], sk[k], AX.X, ALU.add)
                link(ins)
                link(dve.tensor_copy(slot_i[:, 0, :], slot[:, :]))
                dve.tensor_scalar(slot_i[:, 1, :], slot_i[:, 0, :], 7, None, ALU.logical_shift_right)
                link(dve.tensor_scalar(slot_i[:, 2, :], slot_i[:, 0, :], P - 1, None, ALU.bitwise_and))
                dve.tensor_copy(slot_g[:, :], slot_i[:, 1, :])
                link(dve.tensor_copy(slot_p[:, :], slot_i[:, 2, :]))
                dve.tensor_tensor(in_tile[:, :, :], slot_tile[:, :].unsqueeze(1).broadcast_to([P, NC, G]),
                                  slot_g[:, :].unsqueeze(2).broadcast_to([P, NC, G]), ALU.is_equal
                                  ).then_inc(in_tile_ready, 1)
                sh_lo(layer, 0, 1 + 2 * layer)
                dve.wait_ge(in_tile_ready, layer + 1)
                dve.tensor_scalar(in_tile_id[:, :, 1, :], in_tile[:, :, :], own_lane[:, 0:1], None, ALU.mult
                                  ).then_inc(lane_ids_ready, 1)
                for half in range(2):
                    at = slice(half * NC // 2, (half + 1) * NC // 2)
                    dve.tensor_tensor(in_lane[:, at, :], lane[:, :].unsqueeze(1).broadcast_to([P, NC // 2, P]),
                                      slot_p[:, at].unsqueeze(2).broadcast_to([P, NC // 2, P]), ALU.is_equal
                                      ).then_inc(in_lane_ready, 1)
                    sh_lo(layer, layer, half + (0 if layer else 2))
                link(dve.tensor_tensor(ended[:, :, :], slot_tile[:, :].unsqueeze(2).broadcast_to([P, G, E]),
                                       tile_end[:, :].unsqueeze(1).broadcast_to([P, G, E]), ALU.is_ge))
                link(dve.tensor_reduce(rt[:, 4, :], ended[:, :, :], AX.X, ALU.add))
                dve.tensor_scalar(tile_expert[:, :], rt[:, 4, :], float(E - 1), None, ALU.min
                                  ).then_inc(experts_ready, 1)
                if layer:
                    sh_lo(layer, 1, 2)
                dve.wait_ge(held_ready, layer + 1)
                link(dve.tensor_copy(held[:, :, :].rearrange("p s g -> p (s g)"), bank(6, 2 * G)))
                link(dve.scalar_tensor_tensor(row_id[:, :], held[:, 0, :], float(P), held[:, 1, :], ALU.mult, ALU.add))
                link(dve.tensor_scalar(rt[:, 0, :], row_id[:, :], -float(P), None, ALU.add))
                dve.tensor_scalar(rt[:, 1, :], rt[:, 0, :], float(N), -float(N), ALU.is_ge, ALU.mult)
                link(dve.scalar_tensor_tensor(rt[:, 2, :], rt[:, 0, :], 0.0, spare_row[:, :], ALU.is_lt, ALU.mult))
                dve.tensor_tensor(scatter_row[:, :], rt[:, 0, :], rt[:, 2, :], ALU.add)
                link(dve.tensor_tensor(rt[:, 3, :], rt[:, 0, :], rt[:, 1, :], ALU.add))
                dve.tensor_scalar(gather_row[:, :], rt[:, 3, :], 0.0, None, ALU.max).then_inc(rows_ready, 1)

            def make_gates(layer):
                dve.wait_ge(gap_tanh_ready, layer + 1)
                dve.tensor_scalar(gate[:, 0, :], gap_tanh[:, :], -0.25, 0.25, ALU.mult, ALU.add)
                link(dve.tensor_scalar(gate[:, 1, :], gap_tanh[:, :], 0.25, 0.25, ALU.mult, ALU.add))
                for k in range(K):
                    ins = dve.tensor_tensor(gates_k[:, k], chosen[:, k],
                                            gate[:, k, :].unsqueeze(2).broadcast_to([P, NT, E]), ALU.mult)
                link(ins)
                dve.tensor_tensor(gates[:, :, 0:E], gates_k[:, 0], gates_k[:, 1], ALU.add).then_inc(gates_ready, 1)

            def routed_tiles(layer):
                def add_b1(i, par, e):
                    dve.wait_ge(up_ready, layer * G + i + 1)
                    dve.scalar_tensor_tensor(up_sum[:, par, :], bank(par), un[:, 2:3], b1_all[:, ds(e * HID, HID)],
                                             ALU.mult, ALU.add).then_inc(sum_ready, 1)

                def expert_regs(first, n):
                    dve.load(regs[0:n], tile_expert[0:1, ds(first, n)])
                    return [dve.snap(r, min_val=0, max_val=E - 1) for r in regs[0:n]]

                def low(i, par):
                    dve.wait_ge(high_ready, layer * G + i + 1)
                    dve.scalar_tensor_tensor(hs[:, par, 1, :], bank(2 + par), scale_w[:, 6:7], hs[:, par, 0, :],
                                             ALU.mult, ALU.subtract).then_inc(split_ready, 1)

                def sum_y(i, k, sent):
                    if layer or sent is not None:
                        dve.wait_ge(scattered[k], 16 * (layer * RUNS[k] + (0 if sent is None else sent)))
                    dve.wait_ge(y_low_ready, layer * G + i + 1)
                    dve.tensor_tensor(y[:, k, :], bank(4 + k % 2, C), y_low[:, k % 2, :], ALU.add).then_inc(y_ready, 1)

                def body(n, sent):
                    last = isinstance(n, int) and n == BODIES - 1
                    tiles_here = G - LAST if last else U
                    for k in range(tiles_here):
                        i = n * U + k
                        if not last or k + 1 < tiles_here:
                            low(i + 1, (k + 1) % 2)
                        if k == 0:
                            e = expert_regs(n * U + 3, tiles_here - 3 if last else U)
                        if not last or k + 3 < tiles_here:
                            add_b1(i + 3, (k + 1) % 2, e[k])
                        sum_y(i, k, sent)

                if layer == 0:
                    dve.wait_ge(b1_loaded, 16)
                e = expert_regs(0, 3)
                dve.wait_ge(sh_split, NB * J * (layer + 1))
                add_b1(0, 0, e[0])
                add_b1(1, 1, e[1])
                sh_add(layer, NB - 1)
                low(0, 0)
                add_b1(2, 0, e[2])
                body(0, None)
                with dve.Fori(1, BODIES - 1) as n:
                    body(n, n)
                body(BODIES - 1, BODIES - 1)

            def add_biases(layer):
                for g in range(NB):
                    at = slice(g * T_SEQ, (g + 1) * T_SEQ)
                    dve.wait_ge(bias_ready, layer * NB + g + 1)
                    ins = dve.tensor_tensor(xs[:, at], xs[:, at], bank(BIAS_BANKS[g]), ALU.add)
                link(ins)

            def combine(layer, g):
                at = slice(g * T_SEQ, (g + 1) * T_SEQ)
                dve.wait_ge(routed_back[g], 16 * K * (layer + 1))
                for k in range(K):
                    if k in ACT_GATES[layer][g]:
                        dve.wait_ge(products_ready, layer * NB + g + 1)
                        ins = dve.tensor_tensor(xs[:, at], xs[:, at], routed[:, k * N + g * T_SEQ:k * N + (g + 1) * T_SEQ],
                                                ALU.add)
                    else:
                        for t in range(g * TG, (g + 1) * TG):
                            row = slice(t * C, (t + 1) * C)
                            ins = dve.scalar_tensor_tensor(xs[:, row], routed[:, k * N + t * C:k * N + (t + 1) * C],
                                                           gate_un[:, k, t:t + 1], xs[:, row], ALU.mult, ALU.add)
                    if k == 0:
                        link(ins)
                return ins

            def att_stats(g):
                at = slice(g * TG, (g + 1) * TG)
                link(add_stats(g))
                link(dve.tensor_scalar(att_q[:, 0, at], moments[:, at, 1], EPS, None, ALU.add))
                link(dve.reciprocal(att_v[:, 0, at], att_q[:, 0, at]))
                link(dve.tensor_tensor(att_v[:, 1, at], moments[:, at, 1], att_v[:, 0, at], ALU.mult))
                dve.tensor_scalar(att_q[:, 1, at], att_v[:, 1, at], EPS, None, ALU.add).then_inc(att_var_ready, 1)

            def gru():
                def first_norm(b):
                    dve.wait_ge(att_rstd_ready, b + 1)
                    normalize(xatt, att_r[:, 0], b).then_inc(xatt_ready, 1)

                def scan(b):
                    par = b % 2
                    dve.wait_ge(cand_in, b + 1)
                    dve.wait_ge(z_ready, b + 1)
                    if b >= 2:
                        dve.wait_ge(h_turned, b - 1)
                    link(dve.scalar_tensor_tensor(bt[:, par], bank((2, 6)[par]), cols[:, 3:4], zt[:, par],
                                                  ALU.add, ALU.mult))
                    dve.tensor_tensor_scan(ht[:, par], at_[:, par], bt[:, par], 0.0, ALU.mult,
                                           ALU.add).then_inc(hT_ready, 1)

                def add_states(b):
                    dve.wait_ge(h_turned, b + 1)
                    dve.wait_ge(x_sum_ready, b + 1)
                    link(dve.tensor_tensor(xs[:, b * T_SEQ:(b + 1) * T_SEQ], bank(3),
                                           xs[:, b * T_SEQ:(b + 1) * T_SEQ], ALU.add))
                    add_stats(b).then_inc(var_ready, 1)

                def sum_routed(b):
                    link(combine(0, b))
                    att_stats(b)

                sum_routed(0)
                for b in range(1, NB):
                    sum_routed(b)
                    first_norm(b - 1)
                scan(0)
                first_norm(NB - 1)
                add_states(0)
                scan(1)
                for b in range(1, NB):
                    ln_norm(1, b - 1)
                    add_states(b)
                    ln_low(1, b - 1)
                    if b + 1 < NB:
                        scan(b + 1)
                ln_norm(1, NB - 1)
                ln_low(1, NB - 1)
                sh_lo(1, 0, 0)
                sh_lo(1, 0, 1)

            def routed_peaks():
                dve.wait_ge(routed_loaded, 32)
                dve.tensor_reduce(peak[:, 4:5], w1raw[:, 0:E].rearrange("p e h -> p (e h)"), AX.X, ALU.max,
                                  apply_absolute_value=True)
                dve.tensor_reduce(peak[:, 5:6], w2raw[:, 0:E].rearrange("p e j c -> p (e j c)"), AX.X, ALU.max,
                                  apply_absolute_value=True).then_inc(peaks_ready, 1)

            dve.wait_ge(consts_made, 1)
            for g in range(NB):
                dve.wait_ge(x_loaded[g], 16)
                add_stats(g).then_inc(var_ready, 1)
            for g in range(NB):
                ln_norm(0, g)
                if g:
                    ln_low(0, g - 1)
            ln_low(0, NB - 1)
            first_scales()
            split_shared()
            for layer in range(LAYERS):
                route(layer)
                if layer == 0:
                    routed_peaks()
                    routed_scales()
                dve.tensor_scalar(gate_un[:, :, :], gate[:, :, :], un[:, 3:4], None, ALU.mult
                                  ).then_inc(gate_un_ready, 1)
                dve.wait_ge(gate_un_ready, layer + 1)
                shared_rest(layer)
                routed_tiles(layer)
                add_biases(layer)
                if layer == 0:
                    gru()
            for g in range(NB):
                combine(1, g).then_inc(x_done, 1)

        @block.tensor
        def _(pe):
            def transpose_peaks(n, first, rnd):
                pe.wait_ge(peaks_ready, rnd)
                pe.transpose(bank(7)[0:n, 0:P], peak[:, first:first + n], ident[:, :]).then_inc(peaksT_ready, 1)
                pe.wait_ge(peak_diag_ready, rnd)
                pe.matmul(bank(7, n), ones_row[0:n, :], peak_diag[0:n, 0:n], start=True,
                          stop=True).then_inc(peaks_spread, 1)

            def three(out, wh, wl, xh, xl, first, last):
                pe.matmul(out, wh, xh, start=first, stop=False, skip_group_check=True)
                pe.matmul(out, wh, xl, start=False, stop=False, skip_group_check=True)
                return pe.matmul(out, wl, xh, start=False, stop=last, skip_group_check=True)

            regs = [pe.alloc_register(f"expert_{k}") for k in range(U + 3)]
            pe.wait_ge(consts_made, 1)

            def prepare_weights():
                transpose_peaks(4, 0, 1)
                pe.wait_ge(small_loaded, 16 * (SMALL + 1))
                pe.transpose(bank(0, (E + 1) * J), b1rows[:, :], ident[0:(E + 1) * J, 0:(E + 1) * J])
                pe.transpose(bank(1)[:, 0:C], w_att_raw[:, 0], ident[:, :])
                pe.transpose(bank(1)[:, C:2 * C], w_att_raw[:, 1], ident[:, :]).then_inc(att_w_turned, 1)

            def sh_first(layer, g, j):
                three(bank(j), w1[:, E, 0, j * P:(j + 1) * P], w1[:, E, 1, j * P:(j + 1) * P],
                      xT[:, 0, g * T_SEQ:(g + 1) * T_SEQ], xT[:, 1, g * T_SEQ:(g + 1) * T_SEQ], True, True
                      ).then_inc(sh_up, 1)

            def sh_second(layer, g, j):
                pe.wait_ge(sh_split, layer * NB * J + g * J + j + 1)
                for t in range(TG):
                    hh, hl = (hs_sh[:, s, j, t * P:(t + 1) * P] for s in range(2))
                    ins = three(bank(4 + g % 2)[:, t * C:(t + 1) * C], hh, hl, w2[:, E, j, 0], w2[:, E, j, 1],
                                j == 0 and t == 0, j == J - 1)
                if j == J - 1:
                    ins.then_inc(sh_down, 1)

            def turn_x(layer, g):
                pe.wait_ge(xsplit_ready, layer * NB + g + 1)
                if g >= 2:
                    pe.wait_ge(xT_ready, layer * NB + g - 1)
                for s in range(2):
                    for t in range(TG):
                        ins = pe.transpose(bank(4 + g % 2).bitcast(F16)[:, s * T_SEQ + t * P:s * T_SEQ + (t + 1) * P],
                                           xsplit[:, g * TG + t, s, :], ident16[:, :])
                ins.then_inc(xT_turned, 1)

            def router(layer, g):
                pe.wait_ge(xT_ready, layer * NB + g + 1)
                for t in range(g * TG, (g + 1) * TG):
                    at = slice(t * 2 * E, (t + 1) * 2 * E)
                    pe.matmul(bank(7)[:, at], xT[:, 0, t * P:(t + 1) * P], wr16[:, :, :].rearrange("p s e -> p (s e)"),
                              start=True, stop=False)
                    ins = pe.matmul(bank(7)[:, at], xT[:, 1, t * P:(t + 1) * P],
                                    wr16[:, :, :].rearrange("p s e -> p (s e)"), start=False, stop=True)
                ins.then_inc(logits_ready, 1)

            for g in range(NB):
                turn_x(0, g)
            prepare_weights()
            pe.wait_ge(router_w_ready, 1)
            for g in range(NB):
                router(0, g)

            for layer in range(LAYERS):
                def held_pairs():
                    pe.wait_ge(pair_ids_ready, layer + 1)
                    pe.wait_ge(lane_ids_ready, layer + 1)
                    for n in range(NC):
                        if n % (NC // 2) == 0:
                            pe.wait_ge(in_lane_ready, layer * 2 + n // (NC // 2) + 1)
                        ins = pe.matmul(bank(6, 2 * G), in_lane[:, n, :], in_tile_id[:, n].rearrange("p s g -> p (s g)"),
                                        start=(n == 0), stop=(n == NC - 1))
                    ins.then_inc(held_ready, 1)

                def turn(i, k, sent):
                    pe.wait_ge(gathered[k % U], 16 * (layer * RUNS[k % U] + sent))
                    for s in range(2):
                        ins = pe.transpose(bank(6 + k % 2, P).bitcast(F16)[:, s * P:(s + 1) * P],
                                           xg[:, ds(i * 2 * C + s * C, C)], ident16[:, :])
                    ins.then_inc(xg_turned, 1)

                def up(i, par, e):
                    pe.wait_ge(xgT_ready, layer * G + i + 1)
                    wh, wl = (w1f[:, ds(e * (2 * HID) + s * HID, HID)] for s in range(2))
                    xh, xl = xgT[:, par, 0:P], xgT[:, par, P:2 * P]
                    pe.matmul(bank(par), xh, wh, start=True, stop=False)
                    pe.matmul(bank(par), xl, wh, start=False, stop=False)
                    pe.matmul(bank(par), xh, wl, start=False, stop=True).then_inc(up_ready, 1)

                def turn_h(i, par):
                    for j in range(J):
                        if j % (J // 2) == 0:
                            pe.wait_ge(gelu_ready, 2 * (layer * G) + 2 * i + 1 + j // (J // 2))
                        ins = pe.transpose(bank(2 + par)[:, j * P:(j + 1) * P], h[:, par, j * P:(j + 1) * P],
                                           ident[:, :])
                    ins.then_inc(h_slots_turned, 1)

                def down(i, par, e):
                    pe.wait_ge(split_ready, layer * G + i + 1)
                    for j in range(J):
                        hh, hl = (hs[:, par, s, j * P:(j + 1) * P] for s in range(2))
                        at = e * (2 * HID) + j * 2 * C
                        pe.matmul(bank(4 + par, 2 * C), hh, w2f[:, ds(at, 2 * C)], start=(j == 0), stop=False,
                                  skip_group_check=True)
                        ins = pe.matmul(bank(4 + par, C), hl, w2f[:, ds(at, C)], start=False, stop=(j == J - 1),
                                        skip_group_check=True)
                    ins.then_inc(down_ready, 1)

                def expert_regs(first, n, regs):
                    pe.load(regs[0:n], tile_expert[0:1, ds(first, n)])
                    return [pe.snap(r, min_val=0, max_val=E - 1) for r in regs[0:n]]

                if layer == 0:
                    pe.wait_ge(weights_split, 1)
                for j in range(2 * layer, J):
                    sh_first(layer, 0, j)
                pe.wait_ge(used_ready, layer + 1)
                pe.matmul(bank(6, P), before[:, :], used[:, :], start=True, stop=False)
                pe.matmul(bank(6, P), ones16[:, :], ahead[:, :], start=False, stop=True)
                pe.matmul(bank(6)[:, P:P + E], ones16[:, :], total[:, :], start=True, stop=True).then_inc(rank_ready, 1)
                for g in range(NB - 1):
                    if layer == 0 and g == 1:
                        transpose_peaks(2, 4, 2)
                    for j in range(J):
                        if (g, j) == HELD_AT[layer]:
                            held_pairs()
                        sh_second(layer, g, j)
                        sh_first(layer, g + 1, j)
                sh_second(layer, NB - 1, 0)
                pe.wait_ge(experts_ready, layer + 1)
                pe.wait_ge(rows_ready, layer + 1)
                if layer == 0:
                    pe.wait_ge(weights_low, 1)
                e = expert_regs(0, 3, regs)
                turn(0, 0, 1)
                turn(1, 1, 1)
                sh_second(layer, NB - 1, 1)
                up(0, 0, e[0])
                sh_second(layer, NB - 1, 2)
                up(1, 1, e[1])
                turn(2, 2, 1)
                sh_second(layer, NB - 1, 3)

                turn_h(0, 0)
                turn(3, 3, 1)
                up(2, 0, e[2])
                with pe.Fori(0, BODIES - 1) as n:
                    for k in range(U):
                        turn_h(n * U + k + 1, (k + 1) % 2)
                        if k == 0:
                            e = expert_regs(n * U, U + 3, regs)
                        down(n * U + k, k % 2, e[k])
                        turn(n * U + k + 4, k + 4, n + 1 + (k + 4) // U)
                        up(n * U + k + 3, (k + 1) % 2, e[k + 3])
                e = expert_regs(LAST, G - LAST, regs)
                for k in range(G - LAST):
                    i = LAST + k
                    if i + 1 < G:
                        turn_h(i + 1, (k + 1) % 2)
                    down(i, k % 2, e[k])
                    if i + 4 < G:
                        turn(i + 4, k + 4, BODIES)
                    if i + 3 < G:
                        up(i + 3, (k + 1) % 2, e[k + 3])

                pe.wait_ge(gates_ready, layer + 1)
                for g in range(NB):
                    for t in range(TG):
                        ins = pe.transpose(bank(GATE_BANKS[g])[0:E + 1, t * P:(t + 1) * P], gates[:, g * TG + t, :],
                                           ident[:, :])
                    ins.then_inc(gates_turned, 1)
                for g in range(NB):
                    pe.wait_ge(gatesT_ready, layer * NB + g + 1)
                    for t in range(TG):
                        ins = pe.matmul(bank(BIAS_BANKS[g])[:, t * P:(t + 1) * P],
                                        gatesT[:, (g * TG + t) * P:(g * TG + t + 1) * P], b2rows[:, :], start=True,
                                        stop=True)
                    ins.then_inc(bias_ready, 1)

                if layer == 0:
                    def turn_norm(b):
                        pe.wait_ge(norm_ready, b + 1)
                        for t in range(TG):
                            ins = pe.transpose(bank(0)[:, t * P:(t + 1) * P],
                                               xn[:, b * T_SEQ + t * C:b * T_SEQ + (t + 1) * C], ident[:, :])
                        ins.then_inc(norm_turned, 1)

                    def gate_products(b):
                        pe.wait_ge(normT_ready, b + 1)
                        if b:
                            pe.wait_ge(tanh_ready, b)
                        pe.matmul(bank(1), w_att[:, 0], normT[:, b % 2], start=True, stop=True).then_inc(gates_in, 1)
                        if b >= 2:
                            pe.wait_ge(hT_ready, b - 1)
                        pe.matmul(bank((2, 6)[b % 2]), w_att[:, 1], normT[:, b % 2], start=True,
                                  stop=True).then_inc(cand_in, 1)

                    def turn_states(b):
                        pe.wait_ge(hT_ready, b + 1)
                        if b:
                            pe.wait_ge(var_ready, NB + b)
                        for t in range(TG):
                            ins = pe.transpose(bank(3)[:, t * P:(t + 1) * P], ht[:, b % 2, t * P:(t + 1) * P],
                                               ident[:, :])
                        ins.then_inc(h_turned, 1)

                    turn_norm(0)
                    gate_products(0)
                    turn_norm(1)
                    gate_products(1)
                    turn_norm(2)
                    turn_states(0)
                    gate_products(2)
                    turn_norm(3)
                    turn_states(1)
                    gate_products(3)
                    turn_x(1, 0)
                    turn_states(2)
                    router(1, 0)
                    turn_x(1, 1)
                    turn_states(3)
                    pe.wait_ge(tanh_ready, NB)
                    sh_first(1, 0, 0)
                    sh_first(1, 0, 1)
                    router(1, 1)
                    for g in range(2, NB):
                        turn_x(1, g)
                        router(1, g)


_INS = ["L0_attn_x", "L0_attn_gamma", "L0_attn_beta", "L0_attn_Wg", "L0_attn_bg", "L0_attn_Wc", "L0_attn_bc",
        "L0_ffn_Wfc_s", "L0_ffn_bfc_s", "L0_ffn_Wproj_s", "L0_ffn_bproj_s", "L0_ffn_Wr", "L0_ffn_Wfc", "L0_ffn_bfc",
        "L0_ffn_Wproj", "L0_ffn_bproj"]


def kernel(**inputs):
    import numpy as np
    import concourse.bacc as bacc
    from concourse.bass_utils import run_bass_kernel_spmd

    nc = bacc.Bacc("TRN2", target_bir_lowering=False, num_devices=1)
    arrays, args = {}, []
    for name in _INS:
        a = np.ascontiguousarray(inputs[name])
        arrays[f"in_{name}"] = a
        args.append(nc.dram_tensor(f"in_{name}", a.shape, mybir.dt.from_np(a.dtype), kind="ExternalInput").ap())
    out = nc.dram_tensor("out_x", (NB, T_SEQ, C), F32, kind="ExternalOutput").ap()
    macaron(nc, *args, out)
    r = run_bass_kernel_spmd(nc, [arrays], core_ids=[0])
    return r.results[0]["out_x"]
```
